# Optimizing a Trainium2 kernel written in Bass

```python
import numpy as np
import jax
import jax.numpy as jnp

def _softmax(x, axis=-1):
    return jax.nn.softmax(x, axis=axis)
def _gelu(x):
    return jax.nn.gelu(x, approximate=True)
def _silu(x):
    return jax.nn.silu(x)
def _sigmoid(x):
    return jax.nn.sigmoid(x)
def _layernorm(x, axis=-1, eps=1e-5):
    m = jnp.mean(x, axis=axis, keepdims=True)
    v = jnp.var(x, axis=axis, keepdims=True)
    return (x - m) / jnp.sqrt(v + eps)
def _scatter_add(tgt, idx, src, axis=0):
    return tgt.at[idx].add(src)
def _segment_sum(src, seg, n):
    return jax.ops.segment_sum(src, seg, n)

kernel_name = 'mk_conv_preact_d1_conv_nchw96_e8293f'

def setup_inputs(seed: int = 0):
    np.random.seed(seed)
    _w = jnp.asarray
    def _rec_inputs():
        import jax
        import jax.numpy as jnp
        _gk = jax.random.key(seed)
        x = -0.0002221 + 1 * jax.random.normal(jax.random.fold_in(_gk, 1), (16, 96, 128, 128), jnp.float32)
        return x
    x = _rec_inputs()
    def _L0_conv_setup():
        import jax, jax.numpy as jnp
        import numpy as np
        import math
        ALPHA_MIN, ALPHA_MAX = (0.1, 0.9)

        def _dis_s_np(N):
            s = np.zeros(N, dtype=np.float64)
            s[1] = 1.0
            s[N - 1] = 1.0
            idx = (np.arange(N)[:, None] - np.arange(N)[None, :]) % N
            S = s[idx] + np.diag(np.fft.fft(s).real)
            r = N // 2
            even = 1 - N % 2
            P = np.zeros((N, N))
            P[0, 0] = 1.0
            for i in range(1, r - even + 1):
                P[i, i] = 1 / math.sqrt(2)
                P[i, N - i] = 1 / math.sqrt(2)
            if even:
                P[r, r] = 1.0
            for i in range(r + 1, N):
                P[i, i] = -1 / math.sqrt(2)
                P[i, N - i] = 1 / math.sqrt(2)
            CS = P @ S @ P.T
            h = N // 2 + 1
            ec, vc = np.linalg.eigh(CS[:h, :h])
            es, vs = np.linalg.eigh(CS[h:, h:])
            vc = vc[:, np.argsort(-ec)]
            vs = vs[:, np.argsort(-es)]
            SC2 = P @ np.vstack([vc, np.zeros((N - h, h))])
            SS2 = P @ np.vstack([np.zeros((h, N - h)), vs])
            if N % 2 == 0:
                E = np.zeros((N, N + 1))
                SS2 = np.hstack([SS2, np.zeros((N, 1))])
                E[:, 0:N + 1:2] = SC2
                E[:, 1:N:2] = SS2
                E = np.delete(E, N - 1, axis=1)
            else:
                E = np.zeros((N, N))
                E[:, 0:N + 1:2] = SC2
                E[:, 1:N:2] = SS2
            return E.astype(np.float32)

        def _frft_mat(Np, alpha):
            Evec = jnp.asarray(_dis_s_np(Np), dtype=jnp.complex64)
            even = 1 - Np % 2
            l = np.concatenate([np.arange(Np - 1, dtype=np.float32), np.array([Np - 1 + even], dtype=np.float32)])
            theta = np.pi / 2 * alpha[:, None] * jnp.asarray(l)[None, :]
            phase = jax.lax.complex(jnp.cos(theta), -jnp.sin(theta))
            return Np ** 0.5 * jnp.einsum('ji,bj,jk->bik', Evec, phase.astype(jnp.complex64), Evec)

        def _frft2d(x, Fh, Fw):
            xc = jnp.fft.fftshift(x, axes=(2, 3)).astype(jnp.complex64)
            out = jnp.einsum('bij,bcjk->bcik', Fh, xc)
            out = jnp.einsum('bcij,bjk->bcik', out, Fw)
            return jnp.fft.fftshift(out, axes=(2, 3))

        def _mlp(v, w1, b1, w2, b2):
            return jax.nn.relu(v @ w1.T + b1) @ w2.T + b2

        def _gate(g, half):
            go, gi = (g[:, :half], g[:, half:])
            return jax.nn.sigmoid(go[:, :, None] * gi[:, None, :])

        def _group_conv(x, w, b, pad):
            N, Cin, H, W = x.shape
            Cout = w.shape[1]
            out = jax.lax.conv_general_dilated(x.reshape(1, N * Cin, H, W), w.reshape(N * Cout, Cin, w.shape[3], w.shape[4]), (1, 1), [(pad, pad), (pad, pad)], dimension_numbers=('NCHW', 'OIHW', 'NCHW'), feature_group_count=N)
            return out.reshape(N, Cout, out.shape[2], out.shape[3]) + b[None, :, None, None]

        def _forward(x, conv0_w, conv0_b, conv05_w, conv05_b, conv1_w, conv1_b, conv2_w, conv2_b, alpha_w1, alpha_b1, alpha_w2, alpha_b2, gfreq_w1, gfreq_b1, gfreq_w2, gfreq_b2, gsp_w1, gsp_b1, gsp_w2, gsp_b2, gfft_w1, gfft_b1, gfft_w2, gfft_b2):
            N, C, H, W = x.shape
            C0 = C // 3
            C1 = C - 2 * C0
            x_0, x_05, x_1 = (x[:, :C0], x[:, C0:C - C0], x[:, C - C0:])
            Y0 = _gate(_mlp(x_0.mean((2, 3)), gsp_w1, gsp_b1, gsp_w2, gsp_b2), C0)
            x_0 = _group_conv(x_0, conv0_w[None] * Y0[..., None, None], conv0_b, 1)
            gap = x_05.mean((2, 3))
            alpha = ALPHA_MIN + (ALPHA_MAX - ALPHA_MIN) * jax.nn.sigmoid(_mlp(gap, alpha_w1, alpha_b1, alpha_w2, alpha_b2))[:, 0]
            Y = _gate(_mlp(gap, gfreq_w1, gfreq_b1, gfreq_w2, gfreq_b2), 2 * C1)
            Fre = _frft2d(x_05, _frft_mat(H, alpha), _frft_mat(W, alpha))
            Mix = jnp.concatenate([Fre.real, Fre.imag], axis=1)
            Mix = _group_conv(Mix, conv05_w[None] * Y[..., None, None], conv05_b, 0)
            Fre_out = jax.lax.complex(Mix[:, :C1], Mix[:, C1:])
            IFRFT = jnp.abs(_frft2d(Fre_out, _frft_mat(H, -alpha), _frft_mat(W, -alpha))) / (H * W)
            Y1 = _gate(_mlp(x_1.mean((2, 3)), gfft_w1, gfft_b1, gfft_w2, gfft_b2), 2 * C0)
            fre = jnp.fft.rfft2(x_1)
            mix = jnp.concatenate([fre.real, fre.imag], axis=1)
            mix = _group_conv(mix, conv1_w[None] * Y1[..., None, None], conv1_b, 0)
            x_1 = jnp.fft.irfft2(jax.lax.complex(mix[:, :C0], mix[:, C0:]), s=(H, W))
            out = jnp.concatenate([x_0, IFRFT, x_1], axis=1)
            out = jax.lax.conv_general_dilated(out, conv2_w, (1, 1), [(1, 1), (1, 1)], dimension_numbers=('NCHW', 'OIHW', 'NCHW')) + conv2_b[None, :, None, None]
            return out
        key = jax.random.key(seed)
        N, C, H, W = (16, 96, 128, 128)
        C0 = C // 3
        C1 = C - 2 * C0
        hid = max(8, C1 // 4)
        ks = jax.random.split(key, 24)

        def rn(k, shape, s=0.05):
            return s * jax.random.normal(k, shape, dtype=jnp.float32)
        return {'x': jax.random.normal(ks[0], (N, C, H, W), dtype=jnp.float32), 'conv0_w': rn(ks[1], (C0, C0, 3, 3)), 'conv0_b': rn(ks[2], (C0,)), 'conv05_w': rn(ks[3], (2 * C1, 2 * C1, 1, 1)), 'conv05_b': rn(ks[4], (2 * C1,)), 'conv1_w': rn(ks[5], (2 * C0, 2 * C0, 1, 1)), 'conv1_b': rn(ks[6], (2 * C0,)), 'conv2_w': rn(ks[7], (C, C, 3, 3)), 'conv2_b': rn(ks[8], (C,)), 'alpha_w1': rn(ks[9], (hid, C1)), 'alpha_b1': rn(ks[10], (hid,)), 'alpha_w2': rn(ks[11], (1, hid), 0.5), 'alpha_b2': jnp.zeros((1,), jnp.float32), 'gfreq_w1': rn(ks[12], (hid, C1)), 'gfreq_b1': rn(ks[13], (hid,)), 'gfreq_w2': rn(ks[14], (4 * C1, hid)), 'gfreq_b2': rn(ks[15], (4 * C1,)), 'gsp_w1': rn(ks[16], (hid, C0)), 'gsp_b1': rn(ks[17], (hid,)), 'gsp_w2': rn(ks[18], (2 * C0, hid)), 'gsp_b2': rn(ks[19], (2 * C0,)), 'gfft_w1': rn(ks[20], (hid, C0)), 'gfft_b1': rn(ks[21], (hid,)), 'gfft_w2': rn(ks[22], (4 * C0, hid)), 'gfft_b2': rn(ks[23], (4 * C0,))}
    _L0_conv_all = _L0_conv_setup()
    _L0_conv_in = {k: v for k, v in _L0_conv_all.items() if k in ('conv0_w', 'conv0_b', 'conv05_w', 'conv05_b', 'conv1_w', 'conv1_b', 'conv2_w', 'conv2_b', 'alpha_w1', 'alpha_b1', 'alpha_w2', 'alpha_b2', 'gfreq_w1', 'gfreq_b1', 'gfreq_w2', 'gfreq_b2', 'gsp_w1', 'gsp_b1', 'gsp_w2', 'gsp_b2', 'gfft_w1', 'gfft_b1', 'gfft_w2', 'gfft_b2', )}
    del _L0_conv_all

    return {
        "x": x,
        "L0_conv_conv0_w": _L0_conv_in["conv0_w"],
        "L0_conv_conv0_b": _L0_conv_in["conv0_b"],
        "L0_conv_conv05_w": _L0_conv_in["conv05_w"],
        "L0_conv_conv05_b": _L0_conv_in["conv05_b"],
        "L0_conv_conv1_w": _L0_conv_in["conv1_w"],
        "L0_conv_conv1_b": _L0_conv_in["conv1_b"],
        "L0_conv_conv2_w": _L0_conv_in["conv2_w"],
        "L0_conv_conv2_b": _L0_conv_in["conv2_b"],
        "L0_conv_alpha_w1": _L0_conv_in["alpha_w1"],
        "L0_conv_alpha_b1": _L0_conv_in["alpha_b1"],
        "L0_conv_alpha_w2": _L0_conv_in["alpha_w2"],
        "L0_conv_alpha_b2": _L0_conv_in["alpha_b2"],
        "L0_conv_gfreq_w1": _L0_conv_in["gfreq_w1"],
        "L0_conv_gfreq_b1": _L0_conv_in["gfreq_b1"],
        "L0_conv_gfreq_w2": _L0_conv_in["gfreq_w2"],
        "L0_conv_gfreq_b2": _L0_conv_in["gfreq_b2"],
        "L0_conv_gsp_w1": _L0_conv_in["gsp_w1"],
        "L0_conv_gsp_b1": _L0_conv_in["gsp_b1"],
        "L0_conv_gsp_w2": _L0_conv_in["gsp_w2"],
        "L0_conv_gsp_b2": _L0_conv_in["gsp_b2"],
        "L0_conv_gfft_w1": _L0_conv_in["gfft_w1"],
        "L0_conv_gfft_b1": _L0_conv_in["gfft_b1"],
        "L0_conv_gfft_w2": _L0_conv_in["gfft_w2"],
        "L0_conv_gfft_b2": _L0_conv_in["gfft_b2"],
    }

def reference(x, L0_conv_conv0_w, L0_conv_conv0_b, L0_conv_conv05_w, L0_conv_conv05_b, L0_conv_conv1_w, L0_conv_conv1_b, L0_conv_conv2_w, L0_conv_conv2_b, L0_conv_alpha_w1, L0_conv_alpha_b1, L0_conv_alpha_w2, L0_conv_alpha_b2, L0_conv_gfreq_w1, L0_conv_gfreq_b1, L0_conv_gfreq_w2, L0_conv_gfreq_b2, L0_conv_gsp_w1, L0_conv_gsp_b1, L0_conv_gsp_w2, L0_conv_gsp_b2, L0_conv_gfft_w1, L0_conv_gfft_b1, L0_conv_gfft_w2, L0_conv_gfft_b2):
    import jax
    import jax.numpy as jnp
    def _L0_conv_ref(x, conv0_w, conv0_b, conv05_w, conv05_b, conv1_w, conv1_b, conv2_w, conv2_b, alpha_w1, alpha_b1, alpha_w2, alpha_b2, gfreq_w1, gfreq_b1, gfreq_w2, gfreq_b2, gsp_w1, gsp_b1, gsp_w2, gsp_b2, gfft_w1, gfft_b1, gfft_w2, gfft_b2):
        import jax, jax.numpy as jnp
        import numpy as np
        import math
        ALPHA_MIN, ALPHA_MAX = (0.1, 0.9)

        def _dis_s_np(N):
            s = np.zeros(N, dtype=np.float64)
            s[1] = 1.0
            s[N - 1] = 1.0
            idx = (np.arange(N)[:, None] - np.arange(N)[None, :]) % N
            S = s[idx] + np.diag(np.fft.fft(s).real)
            r = N // 2
            even = 1 - N % 2
            P = np.zeros((N, N))
            P[0, 0] = 1.0
            for i in range(1, r - even + 1):
                P[i, i] = 1 / math.sqrt(2)
                P[i, N - i] = 1 / math.sqrt(2)
            if even:
                P[r, r] = 1.0
            for i in range(r + 1, N):
                P[i, i] = -1 / math.sqrt(2)
                P[i, N - i] = 1 / math.sqrt(2)
            CS = P @ S @ P.T
            h = N // 2 + 1
            ec, vc = np.linalg.eigh(CS[:h, :h])
            es, vs = np.linalg.eigh(CS[h:, h:])
            vc = vc[:, np.argsort(-ec)]
            vs = vs[:, np.argsort(-es)]
            SC2 = P @ np.vstack([vc, np.zeros((N - h, h))])
            SS2 = P @ np.vstack([np.zeros((h, N - h)), vs])
            if N % 2 == 0:
                E = np.zeros((N, N + 1))
                SS2 = np.hstack([SS2, np.zeros((N, 1))])
                E[:, 0:N + 1:2] = SC2
                E[:, 1:N:2] = SS2
                E = np.delete(E, N - 1, axis=1)
            else:
                E = np.zeros((N, N))
                E[:, 0:N + 1:2] = SC2
                E[:, 1:N:2] = SS2
            return E.astype(np.float32)

        def _frft_mat(Np, alpha):
            Evec = jnp.asarray(_dis_s_np(Np), dtype=jnp.complex64)
            even = 1 - Np % 2
            l = np.concatenate([np.arange(Np - 1, dtype=np.float32), np.array([Np - 1 + even], dtype=np.float32)])
            theta = np.pi / 2 * alpha[:, None] * jnp.asarray(l)[None, :]
            phase = jax.lax.complex(jnp.cos(theta), -jnp.sin(theta))
            return Np ** 0.5 * jnp.einsum('ji,bj,jk->bik', Evec, phase.astype(jnp.complex64), Evec)

        def _frft2d(x, Fh, Fw):
            xc = jnp.fft.fftshift(x, axes=(2, 3)).astype(jnp.complex64)
            out = jnp.einsum('bij,bcjk->bcik', Fh, xc)
            out = jnp.einsum('bcij,bjk->bcik', out, Fw)
            return jnp.fft.fftshift(out, axes=(2, 3))

        def _mlp(v, w1, b1, w2, b2):
            return jax.nn.relu(v @ w1.T + b1) @ w2.T + b2

        def _gate(g, half):
            go, gi = (g[:, :half], g[:, half:])
            return jax.nn.sigmoid(go[:, :, None] * gi[:, None, :])

        def _group_conv(x, w, b, pad):
            N, Cin, H, W = x.shape
            Cout = w.shape[1]
            out = jax.lax.conv_general_dilated(x.reshape(1, N * Cin, H, W), w.reshape(N * Cout, Cin, w.shape[3], w.shape[4]), (1, 1), [(pad, pad), (pad, pad)], dimension_numbers=('NCHW', 'OIHW', 'NCHW'), feature_group_count=N)
            return out.reshape(N, Cout, out.shape[2], out.shape[3]) + b[None, :, None, None]

        def _forward(x, conv0_w, conv0_b, conv05_w, conv05_b, conv1_w, conv1_b, conv2_w, conv2_b, alpha_w1, alpha_b1, alpha_w2, alpha_b2, gfreq_w1, gfreq_b1, gfreq_w2, gfreq_b2, gsp_w1, gsp_b1, gsp_w2, gsp_b2, gfft_w1, gfft_b1, gfft_w2, gfft_b2):
            N, C, H, W = x.shape
            C0 = C // 3
            C1 = C - 2 * C0
            x_0, x_05, x_1 = (x[:, :C0], x[:, C0:C - C0], x[:, C - C0:])
            Y0 = _gate(_mlp(x_0.mean((2, 3)), gsp_w1, gsp_b1, gsp_w2, gsp_b2), C0)
            x_0 = _group_conv(x_0, conv0_w[None] * Y0[..., None, None], conv0_b, 1)
            gap = x_05.mean((2, 3))
            alpha = ALPHA_MIN + (ALPHA_MAX - ALPHA_MIN) * jax.nn.sigmoid(_mlp(gap, alpha_w1, alpha_b1, alpha_w2, alpha_b2))[:, 0]
            Y = _gate(_mlp(gap, gfreq_w1, gfreq_b1, gfreq_w2, gfreq_b2), 2 * C1)
            Fre = _frft2d(x_05, _frft_mat(H, alpha), _frft_mat(W, alpha))
            Mix = jnp.concatenate([Fre.real, Fre.imag], axis=1)
            Mix = _group_conv(Mix, conv05_w[None] * Y[..., None, None], conv05_b, 0)
            Fre_out = jax.lax.complex(Mix[:, :C1], Mix[:, C1:])
            IFRFT = jnp.abs(_frft2d(Fre_out, _frft_mat(H, -alpha), _frft_mat(W, -alpha))) / (H * W)
            Y1 = _gate(_mlp(x_1.mean((2, 3)), gfft_w1, gfft_b1, gfft_w2, gfft_b2), 2 * C0)
            fre = jnp.fft.rfft2(x_1)
            mix = jnp.concatenate([fre.real, fre.imag], axis=1)
            mix = _group_conv(mix, conv1_w[None] * Y1[..., None, None], conv1_b, 0)
            x_1 = jnp.fft.irfft2(jax.lax.complex(mix[:, :C0], mix[:, C0:]), s=(H, W))
            out = jnp.concatenate([x_0, IFRFT, x_1], axis=1)
            out = jax.lax.conv_general_dilated(out, conv2_w, (1, 1), [(1, 1), (1, 1)], dimension_numbers=('NCHW', 'OIHW', 'NCHW')) + conv2_b[None, :, None, None]
            return out
        return _forward(x, conv0_w, conv0_b, conv05_w, conv05_b, conv1_w, conv1_b, conv2_w, conv2_b, alpha_w1, alpha_b1, alpha_w2, alpha_b2, gfreq_w1, gfreq_b1, gfreq_w2, gfreq_b2, gsp_w1, gsp_b1, gsp_w2, gsp_b2, gfft_w1, gfft_b1, gfft_w2, gfft_b2)

    def _gn(v, G=32, eps=1e-5):
        B_, C_, H_, W_ = v.shape
        g = v.reshape(B_, G, C_ // G, H_, W_)
        m = jnp.mean(g, axis=(2, 3, 4), keepdims=True)
        s = jnp.var(g, axis=(2, 3, 4), keepdims=True)
        return ((g - m) / jnp.sqrt(s + eps)).reshape(v.shape)

    def _ln_c(v, eps=1e-6):
        m = jnp.mean(v, axis=1, keepdims=True)
        s = jnp.var(v, axis=1, keepdims=True)
        return (v - m) / jnp.sqrt(s + eps)

    def _ln_t(v, eps=1e-5):
        m = jnp.mean(v, axis=-1, keepdims=True)
        s = jnp.var(v, axis=-1, keepdims=True)
        return (v - m) / jnp.sqrt(s + eps)

    def _to_tokens(v):
        B_, C_, H_, W_ = v.shape
        return v.reshape(B_, C_, H_ * W_).transpose(0, 2, 1)
    def _from_tokens(t, like):
        B_, C_, H_, W_ = like.shape
        return t.transpose(0, 2, 1).reshape(B_, C_, H_, W_)

    x = x + _L0_conv_ref(_gn(x), L0_conv_conv0_w, L0_conv_conv0_b, L0_conv_conv05_w, L0_conv_conv05_b, L0_conv_conv1_w, L0_conv_conv1_b, L0_conv_conv2_w, L0_conv_conv2_b, L0_conv_alpha_w1, L0_conv_alpha_b1, L0_conv_alpha_w2, L0_conv_alpha_b2, L0_conv_gfreq_w1, L0_conv_gfreq_b1, L0_conv_gfreq_w2, L0_conv_gfreq_b2, L0_conv_gsp_w1, L0_conv_gsp_b1, L0_conv_gsp_w2, L0_conv_gsp_b2, L0_conv_gfft_w1, L0_conv_gfft_b1, L0_conv_gfft_w2, L0_conv_gfft_b2)
    return x


_drawn_inputs = setup_inputs


def setup_inputs(seed=0):
    import zlib

    import numpy as np

    out = dict(_drawn_inputs(seed))
    spreads = {}
    factors = {'L0_conv_conv05_b': 200.0,
     'L0_conv_conv1_b': 171.973,
     'L0_conv_alpha_w1': 8.0,
     'L0_conv_alpha_b1': 5.594,
     'L0_conv_gfreq_w1': 188.788,
     'L0_conv_gfreq_b1': 64.0,
     'L0_conv_gfreq_w2': 36.962,
     'L0_conv_gfreq_b2': 34.475,
     'L0_conv_gsp_w1': 200.0,
     'L0_conv_gsp_b1': 23.82,
     'L0_conv_gsp_w2': 8.0,
     'L0_conv_gsp_b2': 8.0,
     'L0_conv_gfft_w1': 200.0,
     'L0_conv_gfft_b1': 64.0,
     'L0_conv_gfft_w2': 64.0,
     'L0_conv_gfft_b2': 33.462}
    for name, (base, spread) in spreads.items():
        noise = np.random.default_rng([zlib.crc32(name.encode()), seed]).standard_normal(out[name].shape)
        drawn = base * np.exp(spread * noise) if base else spread * noise
        out[name] = jnp.asarray(drawn.astype(out[name].dtype))
    for name, factor in factors.items():
        out[name] = (out[name] * factor).astype(out[name].dtype)
    return out
```

```python
from contextlib import ExitStack

import numpy as np

import concourse.bass as bass
from concourse import mybir

F32 = mybir.dt.float32
F32R = mybir.dt.float32r
ALU = mybir.AluOpType
ACT = mybir.ActivationFunctionType

N = 128
C = 96
G = C // 3
ROWS = 4
S = N // ROWS
PX = ROWS * N
HW = N * N
NP = 5
EPS = 1e-5
TWO_PI = 6.283185
ROUND = 12582912.0
CHUNK = 4096
PIECE = 512
assert S == G


def eigenvectors():
    import math
    s = np.zeros(N, dtype=np.float64)
    s[1] = 1.0
    s[N - 1] = 1.0
    idx = (np.arange(N)[:, None] - np.arange(N)[None, :]) % N
    shifted = s[idx] + np.diag(np.fft.fft(s).real)
    r = N // 2
    even = 1 - N % 2
    P = np.zeros((N, N))
    P[0, 0] = 1.0
    for i in range(1, r - even + 1):
        P[i, i] = 1 / math.sqrt(2)
        P[i, N - i] = 1 / math.sqrt(2)
    if even:
        P[r, r] = 1.0
    for i in range(r + 1, N):
        P[i, i] = -1 / math.sqrt(2)
        P[i, N - i] = 1 / math.sqrt(2)
    CS = P @ shifted @ P.T
    h = N // 2 + 1
    ec, vc = np.linalg.eigh(CS[:h, :h])
    es, vs = np.linalg.eigh(CS[h:, h:])
    vc = vc[:, np.argsort(-ec)]
    vs = vs[:, np.argsort(-es)]
    SC2 = P @ np.vstack([vc, np.zeros((N - h, h))])
    SS2 = P @ np.vstack([np.zeros((h, N - h)), vs])
    E = np.zeros((N, N + 1))
    SS2 = np.hstack([SS2, np.zeros((N, 1))])
    E[:, 0:N + 1:2] = SC2
    E[:, 1:N:2] = SS2
    return np.delete(E, N - 1, axis=1).astype(np.float32)


def constants():
    f32 = np.float32
    E = eigenvectors().astype(np.float64)
    n = np.arange(N)
    odd = n % 2 == 1
    hil = np.where(odd, 2 / N / np.tan(np.pi * np.where(odd, n, 1) / N), 0.0)
    HT = hil[(n[None, :] - n[:, None]) % N]
    neg = (-n) % N
    flip = np.eye(N)[neg]
    mats = np.stack([np.roll(E, N // 2, axis=1), np.eye(N), HT, flip, HT[:, neg]], axis=1)
    power = np.concatenate([np.arange(N - 1), [N]])
    ones = E.sum(1)
    cols = np.zeros((N, 8))
    cols[:, 0] = cols[:, 1] = power / 2
    cols[:, 2] = cols[:, 3] = power / 4
    cols[:, 4] = ones
    cols[:, 5] = ones / np.sqrt(N)
    cols[:, 6] = np.where(n < G, 0, 1)
    cols[:, 7] = np.where(n < 3 * G, 1, 0)
    sel = np.zeros((C, 3, N))
    for k, src in enumerate((0, G, 2 * G)):
        sel[src + n % G, k, n] = 1
    grp = np.kron(np.eye(C // 3), np.full((3, 3), 1 / 3))
    sgn = np.zeros((N, 2 * G))
    sgn[98] = 1
    sgn[99, :G] = -1
    sgn[99, G:] = 1
    row0 = np.stack([np.eye(N)[0], -hil])
    return {"c_mats": mats.astype(f32), "c_cols": cols.astype(f32), "c_sel": sel.astype(f32),
            "c_grp": grp.astype(f32), "c_sgn": sgn.astype(f32), "c_row0": row0.astype(f32)}


def build(nc, x, out, cs):
    NS = x.shape[0]
    x_rows = x.rearrange("n c h w -> n c (h w)")
    x_img = x[:, G:C].rearrange("n (t c) h w -> n c h t w", t=2)
    x_mix = x_rows[:, G:C].rearrange("n (t c) f -> n c t f", t=2)
    out_rows = out.rearrange("n c h w -> n c (h w)")
    scr = nc.dram_tensor("planes", (2, 2, C, HW), F32, kind="Internal").ap()
    scr_y = scr[:, 0, 0:2 * G].rearrange("b (t c) (h w) -> b c h t w", t=2, w=N)
    scr_h = scr[:, 1, 0:3 * G].rearrange("b (t c) (h w) -> b c h t w", t=3, w=N)
    scr_k = scr[:, 0, 2 * G:2 * G + NP].rearrange("b k (h w) -> b h k w", w=N)

    with ExitStack() as ctx:
        def sb(name, shape, dt=F32):
            return ctx.enter_context(nc.sbuf_tensor(name, shape, dt))

        def sem(name):
            return ctx.enter_context(nc.semaphore(name))

        mats = sb("mats", [N, 5, N])
        ET, EYE, HT, FLIP = (mats[:, k, :] for k in range(4))
        cols = sb("cols", [N, 8])
        w0l = sb("w0l", [N, 3, 2, G])
        w2hi = sb("w2hi", [C, 9, C], F32R)
        w2lo = sb("w2lo", [C, 9, C], F32R)
        b0c = sb("b0c", [N, 1])
        b2c = sb("b2c", [C, 1])
        b1rows = sb("b1rows", [2, G])
        row0 = sb("row0", [2, N])
        w_freq = sb("w_freq", [N, NS, 2 * G])
        w_fft = sb("w_fft", [N, NS, G])
        gate0 = sb("gate0", [N, NS, G])
        tab = sb("tab", [N, NS + 1, 10])
        rb0 = sb("rb0", [N, NS, 2])
        bias_fft = sb("bias_fft", [N, NS])
        cin_hi = sb("cin_hi", [C, N + 2, N + 2], F32R)
        cin_lo = sb("cin_lo", [C, N + 2, N + 2], F32R)
        cur_tab = sb("cur_tab", [N, 10])
        cur_rb = sb("cur_rb", [N, 3, 2])
        cur_bf = sb("cur_bf", [N, 1])
        cur_freq = sb("cur_freq", [N, 2 * G])
        cur_fft = sb("cur_fft", [N, G])
        cur_w0 = sb("cur_w0", [N, 3, 2, G])
        el = sb("el", [N, 2, N])
        gmat = sb("gmat", [N, 3, N])
        prow = sb("prow", [2, 2, 3, N])
        pimg = sb("pimg", [N, 4, N])
        arena = sb("arena", [N, 10400])
        at = [0]

        def carve(*dims):
            size = int(np.prod(dims))
            a = arena[:, at[0]:at[0] + size]
            at[0] += size
            assert at[0] <= 10400
            names = " ".join("abc"[:len(dims)])
            if len(dims) == 1:
                return a
            sizes = {k: d for k, d in zip("abc", dims)}
            return a.rearrange(f"p ({names}) -> p {names}", **sizes)

        chunk = [carve(CHUNK) for _ in range(2)]
        at[0] = 0
        w05l, w1l = carve(2, 2 * G), carve(2, 2 * G)
        sel, grp = carve(3, N), carve(C)
        sgn, b05rows = carve(2 * G), carve(2 * G)
        mlp1, mlp1b = carve(4, 9), carve(4)
        mlp2, mlpgo = carve(6, N), carve(160)
        ones = carve(N)
        hid, hidw = carve(4, NS), carve(NS, 2 * G)
        gi = carve(6, NS)
        cst = carve(3, 2, NS)
        t96 = carve(2, NS)
        gap, dev, vdev, msum = (carve(NS) for _ in range(4))
        alpha = carve(NS)
        turn, whole, trig = carve(4, NS), carve(4, NS), carve(4, NS)
        bsel, bmir = carve(NS, NP), carve(NS)
        gate = [carve(NS, 2 * G) for _ in range(2)]
        w2raw = carve(9, C)
        brow = carve(2 * G)
        setup_end = at[0]
        at[0] = 0
        raw = [carve(2, N) for _ in range(2)]
        mixin = [carve(2, PX) for _ in range(2)]
        x0raw = [carve(2, N) for _ in range(2)]
        xres = [carve(PX) for _ in range(2)]
        x0 = carve(2, N + 2)
        tsb, htsb = carve(2, N), carve(2, N)
        ysb, hsb = carve(2, N), carve(3, N)
        sq = carve(2, PX)
        mixed = carve(PX)
        ost = carve(PX)
        at[0] = 0
        stats = sb("stats", [C, HW // PIECE, 6])
        mv = sb("mv", [C, NS, 2])
        mv1 = sb("mv1", [C, 2])

        banks = [ctx.enter_context(nc.psum_tensor(f"bank{i}", [N, 512], F32)) for i in range(8)]
        ps_c2 = banks[0:2]
        ps_mix, ps_c0, ps_t, ps_y, ps_ht, ps_h = banks[2:8]

        consts_in = sem("consts_in")
        chunk_in = [sem(f"chunk_in{i}") for i in range(2)]
        chunk_used = sem("chunk_used")
        stats_of = sem("stats_of")
        stats_kept = sem("stats_kept")
        stats_end = sem("stats_end")
        setup_in = sem("setup_in")
        dve_link = sem("dve_link")
        ones_sb, mv_sb, vdev_sb, veps_sb = sem("ones_sb"), sem("mv_sb"), sem("vdev_sb"), sem("veps_sb")
        mean_ps, var_ps, sd_sb, gap_sb = sem("mean_ps"), sem("var_ps"), sem("sd_sb"), sem("gap_sb")
        l1_ps, hid_sb, l2_ps, alpha_sb = sem("l1_ps"), sem("hid_sb"), sem("l2_ps"), sem("alpha_sb")
        hidw_sb, go_ps, logit_sb, gate_sb = sem("hidw_sb"), sem("go_ps"), sem("logit_sb"), sem("gate_sb")
        gi_sb = sem("gi_sb")
        turn_sb, trig_sb = sem("turn_sb"), sem("trig_sb")
        mixw_sb, sums_ps, w2hi_sb = sem("mixw_sb"), sem("sums_ps"), sem("w2hi_sb")
        ones_out = sem("ones_out")
        border = sem("border")

        raw_in = [sem(f"raw_in{i}") for i in range(2)]
        mix_in = [sem(f"mix_in{i}") for i in range(2)]
        x0_in = [sem(f"x0_in{i}") for i in range(2)]
        res_in = [sem(f"res_in{i}") for i in range(2)]
        y_out, h_out, px_out, pl_out = sem("y_out"), sem("h_out"), sem("px_out"), sem("pl_out")
        t_ps, t_sb = sem("t_ps"), sem("t_sb")
        ht_ps, ht_sb = sem("ht_ps"), sem("ht_sb")
        y_ps, y_sb = sem("y_ps"), sem("y_sb")
        h_ps, h_sb = sem("h_ps"), sem("h_sb")
        x0_sb, c0_ps, c0_sb = sem("x0_sb"), sem("c0_ps"), sem("c0_sb")
        mix_ps, sq_sb, sum_sb = sem("mix_ps"), sem("sq_sb"), sem("sum_sb")
        abs_sb, fft_sb = sem("abs_sb"), sem("fft_sb")
        hi_sb, lo_sb = sem("hi_sb"), sem("lo_sb")
        c2_ps, px_sb = sem("c2_ps"), sem("px_sb")
        tab_sb, el_sb, g_ps, g_sb = sem("tab_sb"), sem("el_sb"), sem("g_ps"), sem("g_sb")
        row_ps, row_sb, pl_ps, pl_sb = sem("row_ps"), sem("row_sb"), sem("pl_ps"), sem("pl_sb")
        back_sb = sem("back_sb")
        credited = sem("credited")
        turns = sem("turns")

        credits = [(s, 1) for s in (t_ps, t_sb, ht_ps, ht_sb, y_ps, y_sb, h_ps, h_sb, x0_sb, c0_ps,
                                    c0_sb, mix_ps, sq_sb, sum_sb, abs_sb, fft_sb, hi_sb, lo_sb,
                                    c2_ps, px_sb, tab_sb, el_sb, g_ps, g_sb, row_ps, row_sb,
                                    pl_ps, pl_sb, back_sb)]
        credits += [(s, 16) for s in (y_out, h_out, px_out, pl_out)]

        def done(item, per=1):
            return (item + 1) * per + per

        def before(item, per=1):
            return item * per + per

        def strips(eng, step):
            step(0, 0, 0, True, False)
            with eng.Fori(0, (S - 2) // 2) as i:
                step(i * 2 + 1, i, 1, False, False)
                step(i * 2 + 2, i + 1, 0, False, False)
            step(S - 1, (S - 2) // 2, 1, False, True)

        loads = [(mats[:, :, :], cs["c_mats"]), (cols[:, :], cs["c_cols"]),
                 (w0l[:, :, :, :], cs["w0l"]), (b0c[:, :], cs["b0c"]), (b2c[:, :], cs["b2c"]),
                 (b1rows[:, :], cs["b1rows"]), (row0[:, :], cs["c_row0"])]
        set_loads = [(w05l, cs["w05l"]), (w1l, cs["w1l"]), (sel[0:C], cs["c_sel"]),
                     (grp[0:C], cs["c_grp"]), (sgn, cs["c_sgn"]), (b05rows, cs["b05rows"]),
                     (mlp1[0:C], cs["mlp1"]), (mlp1b[0:9], cs["mlp1b"]), (mlp2[0:9], cs["mlp2"]),
                     (mlpgo[0:9], cs["mlpgo"]), (w2raw[0:C], cs["w2l"])]
        NCH = HW // CHUNK
        PER = CHUNK // PIECE
        FC = min(NS, 512 // (2 * G))
        NFC = NS // FC
        WIDTH = (2 * G, 2 * G, G)
        GOBANK = (0, 2, 5)

        block = ctx.enter_context(nc.Block())

        @block.sync
        def _(sp):
            for dst, src in loads:
                sp.dma_start(dst, src).then_inc(consts_in, 16)
            with sp.Fori(0, NS) as n:
                for k in range(NCH):
                    sp.wait_ge(chunk_used, n * NCH + (k + 1))
                    sp.dma_start(chunk[k % 2][0:C], x_rows[n, :, k * CHUNK:(k + 1) * CHUNK])\
                      .then_inc(chunk_in[k % 2], 16)
            sp.wait_ge(stats_end, 1)
            for dst, src in set_loads:
                sp.dma_start(dst, src).then_inc(setup_in, 16)
            sp.wait_ge(ones_sb, 1)
            for par in range(2):
                sp.dma_start(scr_k[par, :, NP - 1, :], ones).then_inc(ones_out, 16)
            sp.wait_ge(credited, 1)

            def load_raw(m, f, c, slot, first):
                if not first:
                    sp.wait_ge(t_ps, f)
                    sp.wait_ge(ht_ps, f)
                sp.dma_start(raw[slot], x_img[m, c]).then_inc(raw_in[slot], 16)

            def load_planes(par, b, s, slot, first):
                if not first:
                    sp.wait_ge(mix_ps, b)
                sp.dma_start(mixin[slot][G:3 * G],
                             scr[par, :, 0:2 * G, bass.ds(s * PX, PX)].rearrange("t q f -> q t f"))\
                  .then_inc(mix_in[slot], 16)
                sp.dma_start(mixin[slot][3 * G:3 * G + NP, 0, :],
                             scr[par, 0, 2 * G:2 * G + NP, bass.ds(s * PX, PX)])\
                  .then_inc(mix_in[slot], 16)
                sp.dma_start(mixin[slot][3 * G:4 * G, 1, :],
                             scr[par, 1, 2 * G:3 * G, bass.ds(s * PX, PX)])\
                  .then_inc(mix_in[slot], 16)

            def load_strip(n, b, s, slot, first, last):
                if not first:
                    sp.wait_ge(mix_ps, b)
                    sp.wait_ge(x0_sb, b)
                sp.dma_start(mixin[slot][0:G], x_mix[n, :, :, bass.ds(s * PX, PX)])\
                  .then_inc(mix_in[slot], 16)
                for r in range(4):
                    p0 = 1 if first and r == 0 else 0
                    p1 = 1 if last and r == 3 else 2
                    if p1 - p0 == 2:
                        odd = r // 2
                        rows = x[n, 0:G, bass.ds(s * ROWS + (r - 1 - odd), 4), :]\
                            .rearrange("c (p t) w -> c p t w", t=2)[:, :, odd, :]
                    else:
                        rows = x[n, 0:G, bass.ds(s * ROWS + (2 * p0 + r - 1), 1), :]
                    sp.dma_start(x0raw[slot][r * G:(r + 1) * G, p0:p1, :], rows)\
                      .then_inc(x0_in[slot], 16)

            def load_residual(n, b, s, slot, first):
                if not first:
                    sp.wait_ge(px_sb, b)
                sp.dma_start(xres[slot][0:C], x_rows[n, :, bass.ds(s * PX, PX)])\
                  .then_inc(res_in[slot], 16)

            def store_channel(par, f, c):
                sp.wait_ge(y_sb, done(f))
                sp.wait_ge(h_sb, done(f))
                sp.sem_inc(turns, 1)
                sp.dma_start(scr_y[par, c], ysb).then_inc(y_out, 16)
                sp.dma_start(scr_h[par, c], hsb).then_inc(h_out, 16)

            def store_planes(m):
                sp.wait_ge(pl_sb, done(m))
                sp.dma_start(scr_k[m % 2, :, 0:4, :], pimg[:, :, :]).then_inc(pl_out, 16)

            def store_strip(n, b, s):
                sp.wait_ge(px_sb, done(b))
                sp.dma_start(out_rows[n, :, bass.ds(s * PX, PX)], ost[0:C]).then_inc(px_out, 16)

            def sample(n, front, back):
                if back:
                    sp.wait_ge(y_out, done(n * S + (S - 1), 16))
                    sp.wait_ge(h_out, done(n * S + (S - 1), 16))
                    sp.wait_ge(pl_out, done(n, 16))
                    load_planes(n % 2, n * S, 0, 0, True)
                    load_strip(n, n * S, 0, 0, True, False)
                m = n + 1 if back else n
                if front:
                    load_raw(m, m * S, 0, 0, True)

                def step(s, half, slot, first, last):
                    if not last:
                        if back:
                            nxt_last = isinstance(s, int) and s + 1 == S - 1
                            load_planes(n % 2, n * S + s + 1, s + 1, 1 - slot, False)
                            load_strip(n, n * S + s + 1, s + 1, 1 - slot, False, nxt_last)
                        if front:
                            load_raw(m, m * S + s + 1, s + 1, 1 - slot, False)
                    if back:
                        load_residual(n, n * S + s, s, slot, first)
                    if front:
                        store_channel(m % 2, m * S + s, s)
                    if back and not first:
                        store_strip(n, n * S + s - 1, s - 1)

                step(0, 0, 0, True, False)
                with sp.Fori(0, (S - 4) // 2) as i:
                    step(i * 2 + 1, i, 1, False, False)
                    step(i * 2 + 2, i + 1, 0, False, False)
                step(S - 3, 0, 1, False, False)
                step(S - 2, 0, 0, False, False)
                step(S - 1, 0, 1, False, True)
                if back:
                    store_strip(n, n * S + (S - 1), S - 1)
                return m

            store_planes(0)
            sample(0, True, False)
            store_planes(1)
            with sp.Fori(0, NS - 1) as n:
                sample(n, True, True)
                store_planes(n + 2)
            sample(NS - 1, False, True)
            sp.wait_ge(y_out, done(NS * S - 1, 16))
            sp.wait_ge(h_out, done(NS * S - 1, 16))
            sp.wait_ge(pl_out, done(NS, 16))
            sp.wait_ge(px_out, done(NS * S - 1, 16))

        @block.tensor
        def _(pe):
            mm = pe.matmul
            pe.wait_ge(setup_in, 16 * len(set_loads))
            pe.wait_ge(consts_in, 16 * len(loads))
            pe.wait_ge(mv_sb, 1)
            mm(banks[0][0:C, 0:NS], grp[0:C], mv[:, :, 0], start=True, stop=True).then_inc(mean_ps, 1)
            pe.wait_ge(vdev_sb, 1)
            mm(banks[1][0:C, 0:NS], grp[0:C], vdev[0:C], start=True, stop=True).then_inc(var_ps, 1)
            pe.wait_ge(gap_sb, 1)
            for k in range(3):
                mm(banks[2][:, k * 2 * NS:(k + 1) * 2 * NS], sel[0:C, k, :], t96[0:C, :, :],
                   start=True, stop=True)
            for k in range(4):
                last = mm(banks[3][0:9, k * NS:(k + 1) * NS], mlp1[0:C, k, :], gap[0:C],
                          start=True, stop=True)
            last.then_inc(l1_ps, 1)
            pe.wait_ge(hid_sb, 1)
            for k, h in enumerate((0, 1, 1, 2, 2, 3)):
                last = mm(banks[4][:, k * NS:(k + 1) * NS], mlp2[0:9, k, :], hid[0:9, h, :],
                          start=True, stop=True)
            last.then_inc(l2_ps, 1)
            for k, f in enumerate(WIDTH):
                pe.wait_ge(hidw_sb, k + 1)
                for j in range(NFC):
                    last = mm(banks[GOBANK[k] + j][:, 0:FC * f], ones[0:9, :],
                              hidw[0:9, j * FC:(j + 1) * FC, 0:f], start=True, stop=True)
                last.then_inc(go_ps, 1)
            pe.wait_ge(mixw_sb, 1)
            for n in range(NS):
                mm(banks[n // FC][C:C + NP, n % FC * 2 * G:(n % FC + 1) * 2 * G],
                   bsel[0:C, n, :], w_freq[0:C, n, :], start=True, stop=True)
            for n in range(NS):
                last = mm(banks[7][2 * G:3 * G, n:n + 1], w_fft[0:C, n, :], bmir[0:C, n:n + 1],
                          start=True, stop=True)
            last.then_inc(sums_ps, 1)
            pe.wait_ge(credited, 1)

            def transforms_in(m, f, slot, uses):
                pe.wait_ge(raw_in[slot], uses * 16)
                pe.wait_ge(t_sb, before(f))
                mm(ps_t[:, 0:2 * N], raw[slot][:, 0, :],
                   gmat[:, 1:3, :], start=True, stop=True).then_inc(t_ps, 1)
                pe.wait_ge(ht_sb, before(f))
                pe.transpose(ps_ht[:, 0:N], raw[slot][:, 1, :], EYE)
                pe.transpose(ps_ht[:, N:2 * N], raw[slot][:, 1, :], FLIP).then_inc(ht_ps, 1)

            def transforms_out(f):
                pe.wait_ge(t_sb, done(f))
                pe.wait_ge(y_sb, before(f))
                mm(ps_y[:, 0:2 * N], tsb[:, 0, :], gmat[:, 1:3, :], start=True, stop=False)
                mm(ps_y[:, 0:2 * N], tsb[:, 1, :], gmat[:, 0:2, :], start=False, stop=True)\
                    .then_inc(y_ps, 1)
                pe.wait_ge(ht_sb, done(f))
                pe.wait_ge(h_sb, before(f))
                mm(ps_h[:, 0:N], htsb[:, 0, :], HT, start=True, stop=True)
                mm(ps_h[:, N:3 * N], htsb[:, 1, :], mats[:, 3:5, :], start=True, stop=True)\
                    .then_inc(h_ps, 1)

            def mixes(b, slot, uses, first):
                pe.wait_ge(x0_sb, done(b))
                pe.wait_ge(c0_sb, before(b))
                for dw in range(3):
                    for p in range(2):
                        last = mm(ps_c0[p * 2 * G:(p + 1) * 2 * G, 0:N],
                                  cur_w0[:, dw].rearrange("p a b -> p (a b)"),
                                  x0[:, p, dw:dw + N], start=(dw == 0), stop=(dw == 2))
                last.then_inc(c0_ps, 1)
                pe.wait_ge(mix_in[slot], uses * 64)
                pe.wait_ge(sq_sb, before(b))
                pe.wait_ge(fft_sb, before(b))
                mm(ps_mix[2 * G:3 * G, :], cur_fft[:, :], mixin[slot][:, 1, :],
                   start=True, stop=not first)
                last = mm(ps_mix[0:2 * G, :], cur_freq[0:C + NP, :], mixin[slot][0:C + NP, 0, :],
                          start=True, stop=True)
                if first:
                    last = mm(ps_mix[2 * G:3 * G, 0:N], b1rows[:, :], row0[:, :],
                              start=False, stop=True)
                last.then_inc(mix_ps, 1)

            def last_conv(b, s, slot, tail=False):
                pe.wait_ge(lo_sb, done(b if tail else b + 1))
                pe.wait_ge(px_sb, b if tail else before(b))
                acc = ps_c2[slot][0:C, :].rearrange("p (r w) -> p r w", w=N)
                k = 0
                for w, cin in ((w2hi, cin_hi), (w2lo, cin_hi), (w2hi, cin_lo)):
                    for tap in range(9):
                        last = mm(acc, w[:, tap, :],
                                  cin[:, bass.ds(s * ROWS + tap // 3, ROWS), tap % 3:tap % 3 + N],
                                  start=(k == 0), stop=(k == 26))
                        k += 1
                last.then_inc(c2_ps, 1)

            def make_g(m):
                pe.wait_ge(el_sb, done(m))
                mm(ps_t[:, 0:2 * N], ET, el[:, :, :], start=True, stop=True).then_inc(g_ps, 1)
                for k, bank in enumerate((ps_y, ps_h)):
                    for j, a in enumerate((0, 2, 1)):
                        last = mm(bank[0:2, j * N:(j + 1) * N], cur_tab[:, 4 * k + a:4 * k + a + 2],
                                  ET, start=True, stop=True)
                last.then_inc(row_ps, 1)

            def make_planes(m):
                pe.wait_ge(row_sb, done(m))
                for k in range(2):
                    last = mm(ps_ht[:, k * 2 * N:(k + 1) * 2 * N], prow[:, k, 0, :],
                              prow[:, k, 1:3, :], start=True, stop=True)
                last.then_inc(pl_ps, 1)

            def sample(n, front, back):
                m = n + 1 if back else n
                if front:
                    pe.wait_ge(g_sb, done(m))
                if back:
                    pe.wait_ge(back_sb, done(n))

                def step(s, half, slot, first, last):
                    if front:
                        transforms_in(m, m * S + s, slot, m * (S // 2) + half + 1)
                    if back:
                        mixes(n * S + s, slot, n * (S // 2) + half + 1, first)
                    if front:
                        transforms_out(m * S + s)
                    if back and not first:
                        last_conv(n * S + s - 1, s - 1, 1 - slot)
                strips(pe, step)

            make_g(0)
            make_planes(0)
            pe.wait_ge(pl_sb, done(0))
            sample(0, True, False)
            pe.wait_ge(y_sb, done(S - 1))
            pe.wait_ge(h_sb, done(S - 1))
            make_g(1)
            make_planes(1)
            with pe.Fori(0, NS - 1) as n:
                pe.wait_ge(pl_sb, done(n + 1))
                sample(n, True, True)
                pe.wait_ge(y_sb, done(n * S + (2 * S - 1)))
                pe.wait_ge(h_sb, done(n * S + (2 * S - 1)))
                make_g(n + 2)
                last_conv(n * S + (S - 1), S - 1, 1, tail=True)
                make_planes(n + 2)
            sample(NS - 1, False, True)
            last_conv((NS - 1) * S + (S - 1), S - 1, 1, tail=True)

        @block.scalar
        def _(act):
            act.wait_ge(setup_in, 16 * len(set_loads))
            act.activation(w2hi[:, :, :], w2raw[0:C], ACT.Copy).then_inc(w2hi_sb, 1)
            act.wait_ge(veps_sb, 1)
            act.activation(vdev[0:C], vdev[0:C], ACT.Sqrt).then_inc(sd_sb, 1)
            act.wait_ge(l1_ps, 1)
            for k in range(4):
                last = act.activation(hid[0:9, k, :], banks[3][0:9, k * NS:(k + 1) * NS], ACT.Relu,
                                      bias=mlp1b[0:9, k:k + 1])
            last.then_inc(hid_sb, 1)
            act.wait_ge(gi_sb, 1)
            act.activation(alpha, gi[:, 0, :], ACT.Sigmoid).then_inc(alpha_sb, 1)
            for k in range(3):
                act.wait_ge(logit_sb, k + 1)
                for v in range(2 if k < 2 else 1):
                    g = gate[v][:, :, 0:WIDTH[k]]
                    last = act.activation(g, g, ACT.Sigmoid)
                last.then_inc(gate_sb, 1)
            act.wait_ge(turn_sb, 1)
            act.activation(trig, turn, ACT.Sin, scale=TWO_PI).then_inc(trig_sb, 1)
            act.wait_ge(credited, 1)

            def copy_g(m):
                act.wait_ge(g_ps, done(m))
                act.activation(gmat[:, 1:3, :], ps_t[:, 0:2 * N], ACT.Copy)
                act.activation(gmat[:, 0, :], ps_t[:, N:2 * N], ACT.Copy, scale=-1.0)\
                   .then_inc(g_sb, 1)

            def sample(n, front, back):
                m = n + 1 if back else n
                if back:
                    act.wait_ge(back_sb, done(n))

                def step(s, half, slot, first, last):
                    b, f = n * S + s, m * S + s
                    if back:
                        act.wait_ge(x0_in[slot], (n * (S // 2) + half + 1) * 64)
                        act.wait_ge(c0_ps, before(b))
                        if first or last:
                            for p in range(2):
                                k = 1 if first and p == 0 else 2 if last and p == 1 else 0
                                op = act.activation(x0[:, p, 1:N + 1], x0raw[slot][:, p, :],
                                                    ACT.Identity, bias=cur_rb[:, k, 1:2],
                                                    scale=cur_rb[:, k, 0:1])
                        else:
                            op = act.activation(x0[:, :, 1:N + 1], x0raw[slot], ACT.Identity,
                                                bias=cur_rb[:, 0, 1:2], scale=cur_rb[:, 0, 0:1])
                        op.then_inc(x0_sb, 1)
                    if front:
                        act.wait_ge(t_ps, done(f))
                        act.wait_ge(y_ps, before(f))
                        act.activation(tsb, ps_t[:, 0:2 * N], ACT.Copy).then_inc(t_sb, 1)
                    if back:
                        act.wait_ge(mix_ps, done(b))
                        act.wait_ge(sum_sb, before(b))
                        act.activation(sq[G:2 * G, 0, :], ps_mix[0:G, :], ACT.Square)
                        act.activation(sq[G:2 * G, 1, :], ps_mix[G:2 * G, :], ACT.Square)\
                           .then_inc(sq_sb, 1)
                    if front:
                        act.wait_ge(y_ps, done(f))
                        act.wait_ge(y_out, before(f, 16))
                        act.activation(ysb, ps_y[:, 0:2 * N], ACT.Copy).then_inc(y_sb, 1)
                    if back:
                        act.wait_ge(sum_sb, done(b))
                        act.wait_ge(lo_sb, before(b))
                        act.activation(mixed[G:2 * G], sq[G:2 * G, 0, :], ACT.Sqrt)\
                           .then_inc(abs_sb, 1)
                strips(act, step)

            copy_g(0)
            sample(0, True, False)
            copy_g(1)
            with act.Fori(0, NS - 1) as n:
                sample(n, True, True)
                copy_g(n + 2)
            sample(NS - 1, False, True)

        @block.gpsimd
        def _(pool):
            pool.memset(cin_hi[:, :, :].bitcast(F32), 0.0)
            pool.memset(cin_lo[:, :, :].bitcast(F32), 0.0).then_inc(border, 1)
            pool.wait_ge(credited, 1)

            def sample(n):
                def step(s, half, slot, first, last):
                    b = n * S + s
                    pool.wait_ge(sq_sb, done(b))
                    pool.wait_ge(abs_sb, before(b))
                    pool.wait_ge(hi_sb, before(b))
                    pool.tensor_tensor(sq[G:2 * G, 0, :], sq[G:2 * G, 0, :], sq[G:2 * G, 1, :],
                                       ALU.add).then_inc(sum_sb, 1)
                    pool.wait_ge(c0_sb, done(b))
                    pool.wait_ge(fft_sb, done(b))
                    pool.wait_ge(abs_sb, done(b))
                    pool.wait_ge(sum_sb, done(b))
                    pool.sem_inc(turns, 1)
                    pool.tensor_copy(cin_hi[:, bass.ds(s * ROWS + 1, ROWS), 1:N + 1],
                                     mixed[0:C].rearrange("p (r w) -> p r w", w=N))\
                        .then_inc(hi_sb, 1)
                strips(pool, step)

            with pool.Fori(0, NS) as n:
                sample(n)

        @block.vector
        def _(dve):
            tt, ts, stt, cp = dve.tensor_tensor, dve.tensor_scalar, dve.scalar_tensor_tensor, dve.tensor_copy
            linked = [0]

            def link(op):
                linked[0] += 1
                op.then_inc(dve_link, 1)
                dve.wait_ge(dve_link, linked[0])

            for k in range(2):
                dve.sem_inc(chunk_used, 1)
            with dve.Fori(0, NS) as n:
                for k in range(NCH):
                    dve.wait_ge(chunk_in[k % 2], (n * (NCH // 2) + (k // 2 + 1)) * 16)
                    for j in range(PER):
                        op = dve.bn_stats(stats[:, k * PER + j, :],
                                          chunk[k % 2][0:C, j * PIECE:(j + 1) * PIECE])
                    op.then_inc(chunk_used, 1)
                dve.wait_ge(chunk_used, (n + 1) * NCH + 2)
                dve.sem_inc(turns, 1)
                dve.bn_aggr(mv1[:, :], stats[:, :, :]).then_inc(stats_of, 1)
                dve.wait_ge(stats_of, n + 1)
                cp(mv[:, n, :], mv1[:, :]).then_inc(stats_kept, 1)
                dve.wait_ge(stats_kept, n + 1)
            dve.sem_inc(stats_end, 1)
            dve.memset(ones, 1.0).then_inc(ones_sb, 1)
            dve.wait_ge(setup_in, 16 * len(set_loads))
            dve.wait_ge(consts_in, 16 * len(loads))
            dve.sem_inc(mv_sb, 1)

            dve.wait_ge(mean_ps, 1)
            link(cp(msum[0:C], banks[0][0:C, 0:NS]))
            link(tt(dev[0:C], mv[:, :, 0], msum[0:C], ALU.subtract))
            link(tt(vdev[0:C], dev[0:C], dev[0:C], ALU.mult))
            tt(vdev[0:C], vdev[0:C], mv[:, :, 1], ALU.add).then_inc(vdev_sb, 1)
            dve.wait_ge(var_ps, 1)
            ts(vdev[0:C], banks[1][0:C, 0:NS], EPS, None, ALU.add).then_inc(veps_sb, 1)
            dve.wait_ge(sd_sb, 1)
            link(dve.reciprocal(t96[0:C, 0, :], vdev[0:C]))
            link(stt(t96[0:C, 1, :], msum[0:C], -1.0, t96[0:C, 0, :], ALU.mult, ALU.mult))
            tt(gap[0:C], dev[0:C], t96[0:C, 0, :], ALU.mult).then_inc(gap_sb, 1)
            dve.wait_ge(l1_ps, 1)
            link(cp(cst, banks[2][:, 0:6 * NS].rearrange("p (a b c) -> p a b c", a=3, b=2)))
            link(cp(rb0[:, :, :], cst[:, 0].rearrange("p a b -> p b a")))
            dve.wait_ge(l2_ps, 1)
            cp(gi, banks[4][:, 0:6 * NS].rearrange("p (a b) -> p a b", a=6)).then_inc(gi_sb, 1)
            dve.wait_ge(gi_sb, 1)

            def per_sample(a, width):
                return a[:, :, None].to_broadcast([a.shape[0], a.shape[1], width])

            dve.wait_ge(hid_sb, 1)
            for k, f in enumerate(WIDTH):
                if k:
                    dve.wait_ge(go_ps, k)
                tt(hidw[0:9, :, 0:f], per_sample(hid[0:9, k + 1, :], f),
                   mlpgo[0:9, None, k * 2 * G:k * 2 * G + f].to_broadcast([9, NS, f]),
                   ALU.mult).then_inc(hidw_sb, 1)
                dve.wait_ge(go_ps, k + 1)
                for v in range(2 if k < 2 else 1):
                    for j in range(NFC):
                        op = tt(gate[v][:, j * FC:(j + 1) * FC, 0:f],
                                banks[GOBANK[k] + j][:, 0:FC * f].rearrange("p (a b) -> p a b", b=f),
                                per_sample(gi[:, 1 + 2 * k + v, j * FC:(j + 1) * FC], f), ALU.mult)
                op.then_inc(logit_sb, 1)
                dve.wait_ge(gate_sb, k + 1)
                if k == 2:
                    link(cp(gate0[:, :, :], gate[0][:, :, 0:G]))
                    continue
                wl = (w05l, w1l)[k]
                for v in range(2):
                    link(stt(gate[v], gate[v], 0.5,
                             wl[:, None, v, :].to_broadcast([N, NS, 2 * G]), ALU.mult, ALU.mult))
                lo, hi = slice(0, G), slice(G, 2 * G)
                A, Cw, B, D = gate[0][:, :, lo], gate[0][:, :, hi], gate[1][:, :, lo], gate[1][:, :, hi]
                g = [slice(q * G, (q + 1) * G) for q in range(4)]
                if k == 0:
                    tt(w_freq[g[0], :, lo], A[g[0]], D[g[0]], ALU.add)
                    tt(w_freq[g[0], :, hi], Cw[g[0]], B[g[0]], ALU.subtract)
                    tt(w_freq[g[1], :, lo], A[g[1]], D[g[1]], ALU.subtract)
                    tt(w_freq[g[1], :, hi], B[g[1]], Cw[g[1]], ALU.add)
                    stt(w_freq[g[2], :, lo], B[g[2]], -1.0, Cw[g[2]], ALU.mult, ALU.subtract)
                    link(tt(w_freq[g[2], :, hi], A[g[2]], D[g[2]], ALU.subtract))
                else:
                    tt(w_fft[g[0], :, :], A[g[0]], D[g[0]], ALU.add)
                    tt(w_fft[g[1], :, :], B[g[1]], Cw[g[1]], ALU.subtract)
                    tt(w_fft[g[2], :, :], A[g[2]], D[g[2]], ALU.subtract)
                    link(tt(w_fft[g[3], :, :], B[g[3]], Cw[g[3]], ALU.add))

            link(dve.memset(bsel, 0.0))
            link(dve.memset(bmir, 0.0))
            bcol = cst[:, 1, 1, :]
            cp(bsel[G:2 * G, :, 0], bcol[G:2 * G])
            cp(bsel[2 * G:3 * G, :, 1], bcol[2 * G:3 * G])
            cp(bsel[0:G, :, 4], bcol[0:G])
            cp(bmir[0:G], cst[0:G, 2, 1, :])
            cp(bmir[2 * G:3 * G], cst[2 * G:3 * G, 2, 1, :]).then_inc(mixw_sb, 1)
            link(tt(brow[C:N], b05rows[C:N], sgn[C:N], ALU.mult))
            dve.wait_ge(sums_ps, 1)
            for j in range(NFC):
                tt(w_freq[C:C + NP, j * FC:(j + 1) * FC, :],
                   banks[j][C:C + NP, 0:FC * 2 * G].rearrange("p (a b) -> p a b", b=2 * G),
                   brow[C:C + NP, None, :].to_broadcast([NP, FC, 2 * G]), ALU.add)
            cp(bias_fft[2 * G:3 * G, :], banks[7][2 * G:3 * G, 0:NS])
            tt(w_freq[0:C], w_freq[0:C], per_sample(cst[0:C, 1, 0, :], 2 * G), ALU.mult)
            link(tt(w_fft[:, :, :], w_fft[:, :, :], per_sample(cst[:, 2, 0, :], G), ALU.mult))

            dve.wait_ge(alpha_sb, 1)
            link(ts(alpha, alpha, 0.8, 0.1, ALU.mult, ALU.add))
            for k in range(4):
                link(ts(turn[:, k, :], alpha, cols[:, k:k + 1], (0.25, 0.0)[k % 2],
                        ALU.mult, ALU.add))
            link(ts(whole, turn, ROUND, None, ALU.add))
            link(ts(whole, whole, ROUND, None, ALU.subtract))
            tt(turn, turn, whole, ALU.subtract).then_inc(turn_sb, 1)
            dve.wait_ge(trig_sb, 1)
            link(dve.memset(tab[:, :, :], 0.0))
            for k in range(2):
                for j in range(4):
                    c = trig[:, 2 * k + j % 2, :]
                    link(ts(tab[:, 0:NS, 4 * k + j], c, cols[:, 4 + k:5 + k],
                            -1.0 if j == 3 else 1.0, ALU.mult, ALU.mult))
            for j in range(2):
                link(cp(tab[:, 0:NS, 8 + j], trig[:, j, :]))
            dve.wait_ge(w2hi_sb, 1)
            link(tt(w2lo[:, :, :], w2raw[0:C], w2hi[:, :, :].bitcast(F32), ALU.subtract))
            dve.wait_ge(ones_out, 32)
            link(dve.memset(x0, 0.0))
            link(dve.memset(x0raw[0], 0.0))
            dve.wait_ge(border, 1)
            for s_, v in credits:
                dve.sem_inc(s_, v)
            dve.sem_inc(credited, 1)

            def table(m):
                dve.wait_ge(row_ps, before(m))
                cp(cur_tab[:, :], tab[:, m, :]).then_inc(tab_sb, 1)
                dve.wait_ge(tab_sb, done(m))
                dve.wait_ge(g_ps, before(m))
                for j in range(2):
                    op = ts(el[:, j, :], ET, cur_tab[:, 8 + j:9 + j], None, ALU.mult)
                op.then_inc(el_sb, 1)

            def plane_rows(m):
                dve.wait_ge(row_ps, done(m))
                dve.wait_ge(pl_ps, before(m))
                for k, bank in enumerate((ps_y, ps_h)):
                    op = cp(prow[:, k].rearrange("p a b -> p (a b)"), bank[0:2, 0:3 * N])
                op.then_inc(row_sb, 1)

            def planes(m):
                dve.wait_ge(pl_ps, done(m))
                dve.wait_ge(pl_out, before(m, 16))
                cp(pimg[:, :, :].rearrange("p a b -> p (a b)"), ps_ht[:, :]).then_inc(pl_sb, 1)

            def weights(n):
                dve.wait_ge(c0_ps, before(n * S))
                dve.wait_ge(mix_ps, before(n * S))
                dve.wait_ge(x0_sb, before(n * S))
                dve.wait_ge(fft_sb, before(n * S))
                cp(cur_freq[0:C + NP, :], w_freq[0:C + NP, n, :])
                cp(cur_fft[:, :], w_fft[:, n, :])
                cp(cur_bf[2 * G:3 * G, :], bias_fft[2 * G:3 * G, bass.ds(n, 1)])
                cp(cur_rb[:, 0, :], rb0[:, n, :])
                for k in range(2):
                    ts(cur_rb[:, 1 + k, :], rb0[:, n, :], cols[:, 6 + k:7 + k], None, ALU.mult)
                for dw in range(3):
                    op = tt(cur_w0[:, dw], w0l[:, dw],
                            gate0[:, n, None, :].to_broadcast([N, 2, G]), ALU.mult)
                op.then_inc(back_sb, 1)

            def last_conv(b, slot, uses):
                dve.wait_ge(c2_ps, done(b))
                dve.wait_ge(res_in[slot], uses * 16)
                dve.wait_ge(px_out, before(b, 16))
                stt(ost[0:C], ps_c2[slot][0:C, :], b2c[:, 0:1], xres[slot][0:C],
                    ALU.add, ALU.add).then_inc(px_sb, 1)

            def sample(n, front, back, prepare):
                m = n + 1 if back else n

                def step(s, half, slot, first, last):
                    b, f = n * S + s, m * S + s
                    if front:
                        dve.wait_ge(ht_ps, done(f))
                        dve.wait_ge(h_ps, before(f))
                        cp(htsb.rearrange("p a b -> p (a b)"), ps_ht[:, 0:2 * N]).then_inc(ht_sb, 1)
                    if back:
                        dve.wait_ge(c0_ps, done(b))
                        dve.wait_ge(hi_sb, before(b))
                        dve.wait_ge(lo_sb, before(b))
                        for q in range(ROWS):
                            g = slice(q * G, (q + 1) * G)
                            op = ts(mixed[0:G, q * N:(q + 1) * N], ps_c0[g, 0:N], b0c[g, 0:1], None,
                                    ALU.add)
                        op.then_inc(c0_sb, 1)
                        dve.wait_ge(mix_ps, done(b))
                        ts(mixed[2 * G:3 * G], ps_mix[2 * G:3 * G, :], cur_bf[2 * G:3 * G, 0:1], None,
                           ALU.add).then_inc(fft_sb, 1)
                    if front:
                        dve.wait_ge(h_ps, done(f))
                        dve.wait_ge(h_out, before(f, 16))
                        cp(hsb.rearrange("p a b -> p (a b)"), ps_h[:, 0:3 * N]).then_inc(h_sb, 1)
                    if back:
                        dve.wait_ge(hi_sb, done(b))
                        rows = (slice(None), bass.ds(s * ROWS + 1, ROWS), slice(1, N + 1))
                        tt(cin_lo[rows], mixed[0:C].rearrange("p (r w) -> p r w", w=N),
                           cin_hi[:, :, :].bitcast(F32)[rows], ALU.subtract).then_inc(lo_sb, 1)
                    if last and prepare:
                        table(m + 1)
                    if back and not first:
                        uses = n * (S // 2) + half + (1 if slot == 1 else 0)
                        last_conv(b - 1, 1 - slot, uses)
                strips(dve, step)
                if back and prepare:
                    weights(n + 1)
                    plane_rows(m + 1)
                if back:
                    last_conv(n * S + (S - 1), 1, (n + 1) * (S // 2))
                if back and prepare:
                    planes(m + 1)

            table(0)
            plane_rows(0)
            planes(0)
            sample(0, True, False, True)
            weights(0)
            plane_rows(1)
            planes(1)
            with dve.Fori(0, NS - 1) as n:
                sample(n, True, True, True)
            sample(NS - 1, False, True, False)


def lay_out(inputs):
    w = {k.replace("L0_conv_", ""): np.asarray(v) for k, v in inputs.items() if k != "x"}
    f32 = np.float32
    p = np.arange(N) % G

    def gated(conv):
        t = conv[:, :, 0, 0]
        return np.stack([t[:, v * G + p].T for v in range(2)], axis=1)

    w0l = np.zeros((4, G, 3, 2, G), f32)
    for r in range(4):
        for q in range(2):
            if 0 <= r - q <= 2:
                w0l[r, :, :, q, :] = w["conv0_w"][:, :, r - q, :].transpose(1, 2, 0)
    mlp1 = np.zeros((C, 4, 9), f32)
    mlp1b = np.ones((9, 4), f32)
    for k, (name, at) in enumerate((("alpha", G), ("gfreq", G), ("gfft", 2 * G), ("gsp", 0))):
        mlp1[at:at + G, k, 0:8] = w[name + "_w1"].T
        mlp1b[0:8, k] = w[name + "_b1"]

    def second(name, feature):
        return np.concatenate([w[name + "_w2"][feature].T, w[name + "_b2"][None, feature]])

    mlp2 = np.stack([second("alpha", 0 * p), second("gfreq", 2 * G + p), second("gfreq", 3 * G + p),
                     second("gfft", 2 * G + p), second("gfft", 3 * G + p), second("gsp", G + p)],
                    axis=1)
    mlpgo = np.concatenate([second("gfreq", np.arange(2 * G)), second("gfft", np.arange(2 * G)),
                            second("gsp", np.arange(G))], axis=1)
    b05rows = np.zeros((N, 2 * G), f32)
    b05rows[98] = w["conv05_b"]
    b05rows[99, 0:G] = w["conv05_b"][G:]
    b05rows[99, G:] = w["conv05_b"][:G]
    return {
        "w0l": w0l.reshape(N, 3, 2, G), "w2l": w["conv2_w"].transpose(1, 2, 3, 0).reshape(C, 9, C),
        "b0c": w["conv0_b"][p][:, None], "b2c": w["conv2_b"][:, None],
        "b1rows": w["conv1_b"].reshape(2, G), "w05l": gated(w["conv05_w"]),
        "w1l": gated(w["conv1_w"]), "b05rows": b05rows, "mlp1": mlp1, "mlp1b": mlp1b,
        "mlp2": mlp2, "mlpgo": mlpgo,
    }


def kernel(**inputs):
    import concourse.bacc as bacc
    from concourse.bass_utils import run_bass_kernel_spmd

    nc = bacc.Bacc("TRN2", target_bir_lowering=False, num_devices=1)
    x = np.ascontiguousarray(inputs["x"])
    arrays = {"x": x}
    arrays.update(constants())
    arrays.update({k: np.ascontiguousarray(v) for k, v in lay_out(inputs).items()})
    aps = {k: nc.dram_tensor("in_" + k, a.shape, mybir.dt.from_np(a.dtype), kind="ExternalInput").ap()
           for k, a in arrays.items()}
    out = nc.dram_tensor("out", x.shape, mybir.dt.from_np(x.dtype), kind="ExternalOutput").ap()
    build(nc, aps.pop("x"), out, aps)
    arrays = {"in_" + k: a for k, a in arrays.items()}
    r = run_bass_kernel_spmd(nc, [arrays], core_ids=[0])
    return r.results[0]["out"]
```

```python
from contextlib import ExitStack

import numpy as np

import concourse.bass as bass
from concourse import mybir

F32 = mybir.dt.float32
F32R = mybir.dt.float32r
ALU = mybir.AluOpType
ACT = mybir.ActivationFunctionType

N = 128
C = 96
G = C // 3
ROWS = 4
S = N // ROWS
PX = ROWS * N
HW = N * N
NP = 5
EPS = 1e-5
TWO_PI = 6.283185
ROUND = 12582912.0
CHUNK = 4096
PIECE = 512
LAG = 2
GROUP = 4
RING = GROUP * ROWS + 2
SHIFTS = ((0, 0), (0, 1), (0, 2), (1, 0))
CORNERS = (((0, 0), (0, 1, 2, 3)), ((2, 0), (0, 1, 2)), ((1, 1), (0, 1)))
assert S == G and S % GROUP == 0


def eigenvectors():
    import math
    s = np.zeros(N, dtype=np.float64)
    s[1] = 1.0
    s[N - 1] = 1.0
    idx = (np.arange(N)[:, None] - np.arange(N)[None, :]) % N
    shifted = s[idx] + np.diag(np.fft.fft(s).real)
    r = N // 2
    even = 1 - N % 2
    P = np.zeros((N, N))
    P[0, 0] = 1.0
    for i in range(1, r - even + 1):
        P[i, i] = 1 / math.sqrt(2)
        P[i, N - i] = 1 / math.sqrt(2)
    if even:
        P[r, r] = 1.0
    for i in range(r + 1, N):
        P[i, i] = -1 / math.sqrt(2)
        P[i, N - i] = 1 / math.sqrt(2)
    CS = P @ shifted @ P.T
    h = N // 2 + 1
    ec, vc = np.linalg.eigh(CS[:h, :h])
    es, vs = np.linalg.eigh(CS[h:, h:])
    vc = vc[:, np.argsort(-ec)]
    vs = vs[:, np.argsort(-es)]
    SC2 = P @ np.vstack([vc, np.zeros((N - h, h))])
    SS2 = P @ np.vstack([np.zeros((h, N - h)), vs])
    E = np.zeros((N, N + 1))
    SS2 = np.hstack([SS2, np.zeros((N, 1))])
    E[:, 0:N + 1:2] = SC2
    E[:, 1:N:2] = SS2
    return np.delete(E, N - 1, axis=1).astype(np.float32)


def constants():
    f32 = np.float32
    E = eigenvectors().astype(np.float64)
    n = np.arange(N)
    odd = n % 2 == 1
    hil = np.where(odd, 2 / N / np.tan(np.pi * np.where(odd, n, 1) / N), 0.0)
    HT = hil[(n[None, :] - n[:, None]) % N]
    neg = (-n) % N
    flip = np.eye(N)[neg]
    mats = np.stack([np.roll(E, N // 2, axis=1), np.eye(N), HT, flip, HT[:, neg]], axis=1)
    power = np.concatenate([np.arange(N - 1), [N]])
    ones = E.sum(1)
    cols = np.zeros((N, 8))
    cols[:, 0] = cols[:, 1] = power / 2
    cols[:, 2] = cols[:, 3] = power / 4
    cols[:, 4] = ones
    cols[:, 5] = ones / np.sqrt(N)
    cols[:, 6] = np.where(n < G, 0, 1)
    cols[:, 7] = np.where(n < 3 * G, 1, 0)
    sel = np.zeros((C, 3, N))
    for k, src in enumerate((0, G, 2 * G)):
        sel[src + n % G, k, n] = 1
    grp = np.kron(np.eye(C // 3), np.full((3, 3), 1 / 3))
    sgn = np.zeros((N, 2 * G))
    sgn[98] = 1
    sgn[99, :G] = -1
    sgn[99, G:] = 1
    row0 = np.stack([np.eye(N)[0], -hil])
    return {"c_mats": mats.astype(f32), "c_cols": cols.astype(f32), "c_sel": sel.astype(f32),
            "c_grp": grp.astype(f32), "c_sgn": sgn.astype(f32), "c_row0": row0.astype(f32)}


def build(nc, x, out, cs):
    NS = x.shape[0]
    x_rows = x.rearrange("n c h w -> n c (h w)")
    x_img = x[:, G:C].rearrange("n (t c) h w -> n c h t w", t=2)
    x_mix = x_rows[:, G:C].rearrange("n (t c) f -> n c t f", t=2)
    out_rows = out.rearrange("n c h w -> n c (h w)")
    scr = nc.dram_tensor("planes", (2, 2, C, HW), F32, kind="Internal").ap()
    scr_y = scr[:, 0, 0:2 * G].rearrange("b (t c) (h w) -> b c h t w", t=2, w=N)
    scr_h = scr[:, 1, 0:3 * G].rearrange("b (t c) (h w) -> b c h t w", t=3, w=N)
    scr_k = scr[:, 0, 2 * G:2 * G + NP].rearrange("b k (h w) -> b h k w", w=N)

    with ExitStack() as ctx:
        def sb(name, shape, dt=F32):
            return ctx.enter_context(nc.sbuf_tensor(name, shape, dt))

        def sem(name):
            return ctx.enter_context(nc.semaphore(name))

        mats = sb("mats", [N, 5, N])
        ET, EYE, HT, FLIP = (mats[:, k, :] for k in range(4))
        cols = sb("cols", [N, 8])
        w0l = sb("w0l", [N, 3, 2, G])
        w2a = sb("w2a", [N, 9, C], F32R)
        w2b = sb("w2b", [N, 9, C], F32R)
        w2c = sb("w2c", [N, len(CORNERS), C], F32R)
        b0c = sb("b0c", [N, 1])
        b2c = sb("b2c", [C, 1])
        b1rows = sb("b1rows", [2, G])
        row0 = sb("row0", [2, N])
        w_freq = sb("w_freq", [N, NS, 2 * G])
        w_fft = sb("w_fft", [N, NS, G])
        gate0 = sb("gate0", [N, NS, G])
        tab = sb("tab", [N, NS + 1, 10])
        rb0 = sb("rb0", [N, NS, 2])
        bias_fft = sb("bias_fft", [N, NS])
        ring = sb("ring", [N, 3, RING, N + 2], F32R)
        ring32 = ring[:, :, :, :].bitcast(F32)
        cur_tab = sb("cur_tab", [N, 10])
        cur_rb = sb("cur_rb", [N, 3, 2])
        cur_bf = sb("cur_bf", [N, 1])
        cur_freq = sb("cur_freq", [N, 2 * G])
        cur_fft = sb("cur_fft", [N, G])
        cur_w0 = sb("cur_w0", [N, 3, 2, G])
        el = sb("el", [N, 2, N])
        ghi = sb("ghi", [N, 3, N], F32R)
        glo = sb("glo", [N, 3, N], F32R)
        xhi, xlo = sb("xhi", [N, N], F32R), sb("xlo", [N, N], F32R)
        thi, tlo = sb("thi", [N, 2, N], F32R), sb("tlo", [N, 2, N], F32R)
        prow = sb("prow", [2, 2, 3, N])
        pimg = sb("pimg", [N, 4, N])
        arena = sb("arena", [N, 10400])
        at = [0]

        def carve(*dims):
            size = int(np.prod(dims))
            a = arena[:, at[0]:at[0] + size]
            at[0] += size
            assert at[0] <= 10400
            names = " ".join("abc"[:len(dims)])
            if len(dims) == 1:
                return a
            sizes = {k: d for k, d in zip("abc", dims)}
            return a.rearrange(f"p ({names}) -> p {names}", **sizes)

        chunk = [carve(CHUNK) for _ in range(2)]
        at[0] = 0
        w05l, w1l = carve(2, 2 * G), carve(2, 2 * G)
        sel, grp = carve(3, N), carve(C)
        sgn, b05rows = carve(2 * G), carve(2 * G)
        mlp1, mlp1b = carve(4, 9), carve(4)
        mlp2, mlpgo = carve(6, N), carve(160)
        ones = carve(N)
        hid, hidw = carve(4, NS), carve(NS, 2 * G)
        gi = carve(6, NS)
        cst = carve(3, 2, NS)
        t96 = carve(2, NS)
        gap, dev, vdev, msum = (carve(NS) for _ in range(4))
        alpha = carve(NS)
        turn, whole, trig = carve(4, NS), carve(4, NS), carve(4, NS)
        bsel, bmir = carve(NS, NP), carve(NS)
        gate = [carve(NS, 2 * G) for _ in range(2)]
        w2raw, w2braw = carve(9, C), carve(9, C)
        w2craw = carve(len(CORNERS), C)
        brow = carve(2 * G)
        setup_end = at[0]
        at[0] = 0
        raw = [carve(2, N) for _ in range(2)]
        mixin = [carve(2, PX) for _ in range(2)]
        x0raw = [carve(2, N) for _ in range(2)]
        xres = [carve(PX) for _ in range(2)]
        x0 = carve(2, N + 2)
        htsb = carve(2, N)
        ysb, hsb = carve(2, N), carve(3, N)
        sq = carve(2, PX)
        mixed = carve(PX)
        ost = carve(PX)
        at[0] = 0
        stats = sb("stats", [C, HW // PIECE, 6])
        mv = sb("mv", [C, NS, 2])
        mv1 = sb("mv1", [C, 2])

        banks = [ctx.enter_context(nc.psum_tensor(f"bank{i}", [N, 512], F32)) for i in range(8)]
        ps_c2 = banks[0:2]
        ps_mix, ps_c0, ps_t, ps_y, ps_ht, ps_h = banks[2:8]

        consts_in = sem("consts_in")
        chunk_in = [sem(f"chunk_in{i}") for i in range(2)]
        chunk_used = sem("chunk_used")
        stats_of = sem("stats_of")
        stats_kept = sem("stats_kept")
        stats_end = sem("stats_end")
        setup_in = sem("setup_in")
        dve_link = sem("dve_link")
        ones_sb, mv_sb, vdev_sb, veps_sb = sem("ones_sb"), sem("mv_sb"), sem("vdev_sb"), sem("veps_sb")
        mean_ps, var_ps, sd_sb, gap_sb = sem("mean_ps"), sem("var_ps"), sem("sd_sb"), sem("gap_sb")
        l1_ps, hid_sb, l2_ps, alpha_sb = sem("l1_ps"), sem("hid_sb"), sem("l2_ps"), sem("alpha_sb")
        hidw_sb, go_ps, logit_sb, gate_sb = sem("hidw_sb"), sem("go_ps"), sem("logit_sb"), sem("gate_sb")
        gi_sb = sem("gi_sb")
        turn_sb, trig_sb = sem("turn_sb"), sem("trig_sb")
        mixw_sb, sums_ps, w2hi_sb = sem("mixw_sb"), sem("sums_ps"), sem("w2hi_sb")
        ones_out = sem("ones_out")
        border = sem("border")

        raw_in = [sem(f"raw_in{i}") for i in range(2)]
        mix_in = [sem(f"mix_in{i}") for i in range(2)]
        x0_in = [sem(f"x0_in{i}") for i in range(2)]
        res_in = [sem(f"res_in{i}") for i in range(2)]
        y_out, h_out, px_out, pl_out = sem("y_out"), sem("h_out"), sem("px_out"), sem("pl_out")
        xs_sb, t_ps, th_sb, tl_sb = sem("xs_sb"), sem("t_ps"), sem("th_sb"), sem("tl_sb")
        xh_sb = sem("xh_sb")
        ht_ps, ht_sb = sem("ht_ps"), sem("ht_sb")
        y_ps, y_sb = sem("y_ps"), sem("y_sb")
        h_ps, h_sb = sem("h_ps"), sem("h_sb")
        x0_sb, c0_ps, c0_sb = sem("x0_sb"), sem("c0_ps"), sem("c0_sb")
        mix_ps, sq_sb, sum_sb = sem("mix_ps"), sem("sq_sb"), sem("sum_sb")
        abs_sb, fft_sb = sem("abs_sb"), sem("fft_sb")
        hi_sb, lo_sb, shift_sb = sem("hi_sb"), sem("lo_sb"), sem("shift_sb")
        twin_sb, border_sb = sem("twin_sb"), sem("border_sb")
        c2_ps, px_sb = sem("c2_ps"), sem("px_sb")
        tab_sb, el_sb, g_ps = sem("tab_sb"), sem("el_sb"), sem("g_ps")
        gh_sb, gl_sb = sem("gh_sb"), sem("gl_sb")
        row_ps, row_sb, pl_ps, pl_sb = sem("row_ps"), sem("row_sb"), sem("pl_ps"), sem("pl_sb")
        back_sb = sem("back_sb")
        credited = sem("credited")
        turns = sem("turns")

        credits = [(s, 1) for s in (t_ps, th_sb, tl_sb, xs_sb, xh_sb, ht_ps, ht_sb, y_ps, y_sb, h_ps, h_sb, x0_sb, c0_ps,
                                    c0_sb, mix_ps, sq_sb, sum_sb, abs_sb, fft_sb, hi_sb, lo_sb,
                                    shift_sb, twin_sb, border_sb,
                                    c2_ps, px_sb, tab_sb, el_sb, g_ps, gh_sb, gl_sb, row_ps, row_sb,
                                    pl_ps, pl_sb, back_sb)]
        credits += [(s, 16) for s in (y_out, h_out, px_out, pl_out)]

        def done(item, per=1):
            return (item + 1) * per + per

        def before(item, per=1):
            return item * per + per

        def strips(eng, step):
            for k in range(GROUP):
                step(k, 0, k)
            with eng.Fori(1, S // GROUP - 1) as g:
                for k in range(GROUP):
                    step(g * GROUP + k, g, k)
            for k in range(GROUP):
                step(S - GROUP + k, S // GROUP - 1, k)

        def is_strip(s, which):
            return isinstance(s, int) and s == which

        def uses(image, g, k):
            return image * (S // 2) + (g * 2 + (k // 2 + 1))

        loads = [(mats[:, :, :], cs["c_mats"]), (cols[:, :], cs["c_cols"]),
                 (w0l[:, :, :, :], cs["w0l"]), (b0c[:, :], cs["b0c"]), (b2c[:, :], cs["b2c"]),
                 (b1rows[:, :], cs["b1rows"]), (row0[:, :], cs["c_row0"])]
        set_loads = [(w05l, cs["w05l"]), (w1l, cs["w1l"]), (sel[0:C], cs["c_sel"]),
                     (grp[0:C], cs["c_grp"]), (sgn, cs["c_sgn"]), (b05rows, cs["b05rows"]),
                     (mlp1[0:C], cs["mlp1"]), (mlp1b[0:9], cs["mlp1b"]), (mlp2[0:9], cs["mlp2"]),
                     (mlpgo[0:9], cs["mlpgo"]), (w2raw, cs["w2a"]), (w2braw[C:N], cs["w2b"]),
                     (w2craw, cs["w2c"])]
        NCH = HW // CHUNK
        PER = CHUNK // PIECE
        FC = min(NS, 512 // (2 * G))
        NFC = NS // FC
        WIDTH = (2 * G, 2 * G, G)
        GOBANK = (0, 2, 5)

        def strip(a):
            return a.rearrange("p (r w) -> p r w", w=N)

        def rows(p0, p1, which, k):
            return ring[p0:p1, which, k * ROWS + 1:k * ROWS + 1 + ROWS, 1:N + 1]

        block = ctx.enter_context(nc.Block())

        @block.sync
        def _(sp):
            for dst, src in loads:
                sp.dma_start(dst, src).then_inc(consts_in, 16)
            with sp.Fori(0, NS) as n:
                for k in range(NCH):
                    sp.wait_ge(chunk_used, n * NCH + (k + 1))
                    sp.dma_start(chunk[k % 2][0:C], x_rows[n, :, k * CHUNK:(k + 1) * CHUNK])\
                      .then_inc(chunk_in[k % 2], 16)
            sp.wait_ge(stats_end, 1)
            for dst, src in set_loads:
                sp.dma_start(dst, src).then_inc(setup_in, 16)
            sp.wait_ge(ones_sb, 1)
            for par in range(2):
                sp.dma_start(scr_k[par, :, NP - 1, :], ones).then_inc(ones_out, 16)
            sp.wait_ge(credited, 1)

            def load_raw(m, f, c, slot, first):
                if not first:
                    sp.wait_ge(t_ps, f)
                    sp.wait_ge(ht_ps, f)
                sp.dma_start(raw[slot], x_img[m, c]).then_inc(raw_in[slot], 16)

            def load_planes(par, b, s, slot, first):
                if not first:
                    sp.wait_ge(mix_ps, b)
                sp.dma_start(mixin[slot][G:3 * G],
                             scr[par, :, 0:2 * G, bass.ds(s * PX, PX)].rearrange("t q f -> q t f"))\
                  .then_inc(mix_in[slot], 16)
                sp.dma_start(mixin[slot][3 * G:3 * G + NP, 0, :],
                             scr[par, 0, 2 * G:2 * G + NP, bass.ds(s * PX, PX)])\
                  .then_inc(mix_in[slot], 16)
                sp.dma_start(mixin[slot][3 * G:4 * G, 1, :],
                             scr[par, 1, 2 * G:3 * G, bass.ds(s * PX, PX)])\
                  .then_inc(mix_in[slot], 16)

            def load_strip(n, b, s, slot, first, last):
                if not first:
                    sp.wait_ge(mix_ps, b)
                    sp.wait_ge(x0_sb, b)
                sp.dma_start(mixin[slot][0:G], x_mix[n, :, :, bass.ds(s * PX, PX)])\
                  .then_inc(mix_in[slot], 16)
                for r in range(4):
                    p0 = 1 if first and r == 0 else 0
                    p1 = 1 if last and r == 3 else 2
                    if p1 - p0 == 2:
                        odd = r // 2
                        rows = x[n, 0:G, bass.ds(s * ROWS + (r - 1 - odd), 4), :]\
                            .rearrange("c (p t) w -> c p t w", t=2)[:, :, odd, :]
                    else:
                        rows = x[n, 0:G, bass.ds(s * ROWS + (2 * p0 + r - 1), 1), :]
                    sp.dma_start(x0raw[slot][r * G:(r + 1) * G, p0:p1, :], rows)\
                      .then_inc(x0_in[slot], 16)

            def load_residual(n, b, s, slot, first):
                if not first:
                    sp.wait_ge(px_sb, b)
                sp.dma_start(xres[slot][0:C], x_rows[n, :, bass.ds(s * PX, PX)])\
                  .then_inc(res_in[slot], 16)

            def store_channel(par, f, c):
                sp.wait_ge(y_sb, done(f))
                sp.wait_ge(h_sb, done(f))
                sp.sem_inc(turns, 1)
                sp.dma_start(scr_y[par, c], ysb).then_inc(y_out, 16)
                sp.dma_start(scr_h[par, c], hsb).then_inc(h_out, 16)

            def store_planes(m):
                sp.wait_ge(pl_sb, done(m))
                sp.dma_start(scr_k[m % 2, :, 0:4, :], pimg[:, :, :]).then_inc(pl_out, 16)

            def store_strip(n, b, s):
                sp.wait_ge(px_sb, done(b))
                sp.dma_start(out_rows[n, :, bass.ds(s * PX, PX)], ost[0:C]).then_inc(px_out, 16)

            def sample(n, front, back):
                if back:
                    sp.wait_ge(y_out, done(n * S + (S - 1), 16))
                    sp.wait_ge(h_out, done(n * S + (S - 1), 16))
                    sp.wait_ge(pl_out, done(n, 16))
                    load_planes(n % 2, n * S, 0, 0, True)
                    load_strip(n, n * S, 0, 0, True, False)
                m = n + 1 if back else n
                if front:
                    load_raw(m, m * S, 0, 0, True)

                def step(s, g, k):
                    slot, b = k % 2, n * S + s
                    if not is_strip(s, S - 1):
                        if back:
                            load_planes(n % 2, b + 1, s + 1, 1 - slot, False)
                            load_strip(n, b + 1, s + 1, 1 - slot, False, is_strip(s, S - 2))
                        if front:
                            load_raw(m, m * S + s + 1, s + 1, 1 - slot, False)
                    if back and not is_strip(s, 0):
                        load_residual(n, b - 1, s - 1, 1 - slot, is_strip(s, 1))
                    if front:
                        store_channel(m % 2, m * S + s, s)
                    if back and not (is_strip(s, 0) or is_strip(s, 1)):
                        store_strip(n, b - LAG, s - LAG)
                strips(sp, step)
                if back:
                    load_residual(n, n * S + (S - 1), S - 1, 1, False)
                    for s in range(S - LAG, S):
                        store_strip(n, n * S + s, s)

            store_planes(0)
            sample(0, True, False)
            store_planes(1)
            with sp.Fori(0, NS - 1) as n:
                sample(n, True, True)
                store_planes(n + 2)
            sample(NS - 1, False, True)
            sp.wait_ge(y_out, done(NS * S - 1, 16))
            sp.wait_ge(h_out, done(NS * S - 1, 16))
            sp.wait_ge(pl_out, done(NS, 16))
            sp.wait_ge(px_out, done(NS * S - 1, 16))

        @block.tensor
        def _(pe):
            mm = pe.matmul
            pe.wait_ge(setup_in, 16 * len(set_loads))
            pe.wait_ge(consts_in, 16 * len(loads))
            pe.wait_ge(mv_sb, 1)
            mm(banks[0][0:C, 0:NS], grp[0:C], mv[:, :, 0], start=True, stop=True).then_inc(mean_ps, 1)
            pe.wait_ge(vdev_sb, 1)
            mm(banks[1][0:C, 0:NS], grp[0:C], vdev[0:C], start=True, stop=True).then_inc(var_ps, 1)
            pe.wait_ge(gap_sb, 1)
            for k in range(3):
                mm(banks[2][:, k * 2 * NS:(k + 1) * 2 * NS], sel[0:C, k, :], t96[0:C, :, :],
                   start=True, stop=True)
            for k in range(4):
                last = mm(banks[3][0:9, k * NS:(k + 1) * NS], mlp1[0:C, k, :], gap[0:C],
                          start=True, stop=True)
            last.then_inc(l1_ps, 1)
            pe.wait_ge(hid_sb, 1)
            for k, h in enumerate((0, 1, 1, 2, 2, 3)):
                last = mm(banks[4][:, k * NS:(k + 1) * NS], mlp2[0:9, k, :], hid[0:9, h, :],
                          start=True, stop=True)
            last.then_inc(l2_ps, 1)
            for k, f in enumerate(WIDTH):
                pe.wait_ge(hidw_sb, k + 1)
                for j in range(NFC):
                    last = mm(banks[GOBANK[k] + j][:, 0:FC * f], ones[0:9, :],
                              hidw[0:9, j * FC:(j + 1) * FC, 0:f], start=True, stop=True)
                last.then_inc(go_ps, 1)
            pe.wait_ge(mixw_sb, 1)
            for n in range(NS):
                mm(banks[n // FC][C:C + NP, n % FC * 2 * G:(n % FC + 1) * 2 * G],
                   bsel[0:C, n, :], w_freq[0:C, n, :], start=True, stop=True)
            for n in range(NS):
                last = mm(banks[7][2 * G:3 * G, n:n + 1], w_fft[0:C, n, :], bmir[0:C, n:n + 1],
                          start=True, stop=True)
            last.then_inc(sums_ps, 1)
            pe.wait_ge(credited, 1)

            def transforms_in(f, slot, filled):
                pe.wait_ge(xs_sb, done(f))
                pe.wait_ge(tl_sb, before(f))
                mm(ps_t[:, 0:2 * N], xhi[:, :], ghi[:, 1:3, :], start=True, stop=False)
                mm(ps_t[:, 0:2 * N], xhi[:, :], glo[:, 1:3, :], start=False, stop=False)
                mm(ps_t[:, 0:2 * N], xlo[:, :], ghi[:, 1:3, :], start=False, stop=True)\
                    .then_inc(t_ps, 1)
                pe.wait_ge(raw_in[slot], filled * 16)
                pe.wait_ge(ht_sb, before(f))
                pe.transpose(ps_ht[:, 0:N], raw[slot][:, 1, :], EYE)
                pe.transpose(ps_ht[:, N:2 * N], raw[slot][:, 1, :], FLIP).then_inc(ht_ps, 1)

            def transforms_out(f):
                pe.wait_ge(tl_sb, done(f))
                pe.wait_ge(y_sb, before(f))
                for part in range(2):
                    cut = slice(1 - part, 3 - part)
                    mm(ps_y[:, 0:2 * N], thi[:, part, :], ghi[:, cut, :],
                       start=(part == 0), stop=False)
                    mm(ps_y[:, 0:2 * N], thi[:, part, :], glo[:, cut, :], start=False, stop=False)
                    last = mm(ps_y[:, 0:2 * N], tlo[:, part, :], ghi[:, cut, :],
                              start=False, stop=(part == 1))
                last.then_inc(y_ps, 1)
                pe.wait_ge(ht_sb, done(f))
                pe.wait_ge(h_sb, before(f))
                mm(ps_h[:, 0:N], htsb[:, 0, :], HT, start=True, stop=True)
                mm(ps_h[:, 2 * N:3 * N], htsb[:, 1, :], mats[:, 4, :], start=True, stop=True)
                pe.transpose(ps_h[:, N:2 * N], htsb[:, 1, :], FLIP).then_inc(h_ps, 1)

            def mixes(b, slot, filled, first):
                pe.wait_ge(x0_sb, done(b))
                pe.wait_ge(c0_sb, before(b))
                for dw in range(3):
                    for p in range(2):
                        last = mm(ps_c0[p * 2 * G:(p + 1) * 2 * G, 0:N],
                                  cur_w0[:, dw].rearrange("p a b -> p (a b)"),
                                  x0[:, p, dw:dw + N], start=(dw == 0), stop=(dw == 2))
                last.then_inc(c0_ps, 1)
                pe.wait_ge(mix_in[slot], filled * 64)
                pe.wait_ge(sq_sb, before(b))
                pe.wait_ge(fft_sb, before(b))
                mm(ps_mix[2 * G:3 * G, :], cur_fft[:, :], mixin[slot][:, 1, :],
                   start=True, stop=not first)
                last = mm(ps_mix[0:2 * G, :], cur_freq[0:C + NP, :], mixin[slot][0:C + NP, 0, :],
                          start=True, stop=True)
                if first:
                    last = mm(ps_mix[2 * G:3 * G, 0:N], b1rows[:, :], row0[:, :],
                              start=False, stop=True)
                last.then_inc(mix_ps, 1)

            def last_conv(n, s, g, k, tail=False):
                b = n * S + s
                last_strip = is_strip(s, S - 1)
                pe.wait_ge(shift_sb, done(b if last_strip else b + 1))
                if last_strip:
                    pe.wait_ge(border_sb, done(n))
                elif k == GROUP - 1:
                    pe.wait_ge(twin_sb, done(n * (S // GROUP) + g + 1))
                pe.wait_ge(px_sb, b if tail else before(b))
                acc = ps_c2[k % 2][0:C, :].rearrange("p (r w) -> p r w", w=N)

                def window(which, row, col):
                    return ring[:, which, k * ROWS + row:k * ROWS + row + ROWS, col:col + N]

                for tap in range(9):
                    mm(acc, w2a[:, tap, :], window(0, tap // 3, tap % 3), start=(tap == 0), stop=False)
                for tap in range(9):
                    mm(acc, w2b[:, tap, :], window(1, tap // 3, tap % 3), start=False, stop=False)
                for j, (corner, _) in enumerate(CORNERS):
                    last = mm(acc, w2c[:, j, :], window(2, *corner),
                              start=False, stop=(j == len(CORNERS) - 1))
                last.then_inc(c2_ps, 1)

            def make_g(m):
                pe.wait_ge(el_sb, done(m))
                mm(ps_t[:, 0:2 * N], ET, el[:, :, :], start=True, stop=True).then_inc(g_ps, 1)
                for k, bank in enumerate((ps_y, ps_h)):
                    for j, a in enumerate((0, 2, 1)):
                        last = mm(bank[0:2, j * N:(j + 1) * N], cur_tab[:, 4 * k + a:4 * k + a + 2],
                                  ET, start=True, stop=True)
                last.then_inc(row_ps, 1)

            def make_planes(m):
                pe.wait_ge(row_sb, done(m))
                for k in range(2):
                    last = mm(ps_ht[:, k * 2 * N:(k + 1) * 2 * N], prow[:, k, 0, :],
                              prow[:, k, 1:3, :], start=True, stop=True)
                last.then_inc(pl_ps, 1)

            def sample(n, front, back):
                m = n + 1 if back else n
                if front:
                    pe.wait_ge(gl_sb, done(m))
                if back:
                    pe.wait_ge(back_sb, done(n))

                def step(s, g, k):
                    slot = k % 2
                    if front:
                        transforms_in(m * S + s, slot, uses(m, g, k))
                    if back:
                        mixes(n * S + s, slot, uses(n, g, k), is_strip(s, 0))
                    if front:
                        transforms_out(m * S + s)
                    if back and not (is_strip(s, 0) or is_strip(s, 1)):
                        last_conv(n, s - LAG, g if k >= LAG else g - 1, (k - LAG) % GROUP)
                strips(pe, step)

            make_g(0)
            make_planes(0)
            pe.wait_ge(pl_sb, done(0))
            sample(0, True, False)
            pe.wait_ge(y_sb, done(S - 1))
            pe.wait_ge(h_sb, done(S - 1))
            make_g(1)
            make_planes(1)
            with pe.Fori(0, NS - 1) as n:
                pe.wait_ge(pl_sb, done(n + 1))
                sample(n, True, True)
                last_conv(n, S - 2, S // GROUP - 1, GROUP - 2, tail=True)
                pe.wait_ge(y_sb, done(n * S + (2 * S - 1)))
                pe.wait_ge(h_sb, done(n * S + (2 * S - 1)))
                make_g(n + 2)
                last_conv(n, S - 1, S // GROUP - 1, GROUP - 1, tail=True)
                make_planes(n + 2)
            sample(NS - 1, False, True)
            for k in range(LAG, GROUP):
                last_conv(NS - 1, S - GROUP + k, S // GROUP - 1, k, tail=True)

        @block.scalar
        def _(act):
            act.wait_ge(setup_in, 16 * len(set_loads))
            act.activation(w2a[:, :, :], w2raw, ACT.Copy)
            act.activation(w2b[C:N, :, :], w2braw[C:N], ACT.Copy)
            act.activation(w2c[:, :, :], w2craw, ACT.Copy).then_inc(w2hi_sb, 1)
            act.wait_ge(veps_sb, 1)
            act.activation(vdev[0:C], vdev[0:C], ACT.Sqrt).then_inc(sd_sb, 1)
            act.wait_ge(l1_ps, 1)
            for k in range(4):
                last = act.activation(hid[0:9, k, :], banks[3][0:9, k * NS:(k + 1) * NS], ACT.Relu,
                                      bias=mlp1b[0:9, k:k + 1])
            last.then_inc(hid_sb, 1)
            act.wait_ge(gi_sb, 1)
            act.activation(alpha, gi[:, 0, :], ACT.Sigmoid).then_inc(alpha_sb, 1)
            for k in range(3):
                act.wait_ge(logit_sb, k + 1)
                for v in range(2 if k < 2 else 1):
                    g = gate[v][:, :, 0:WIDTH[k]]
                    last = act.activation(g, g, ACT.Sigmoid)
                last.then_inc(gate_sb, 1)
            act.wait_ge(turn_sb, 1)
            act.activation(trig, turn, ACT.Sin, scale=TWO_PI).then_inc(trig_sb, 1)
            act.wait_ge(credited, 1)

            def copy_g(m):
                act.wait_ge(g_ps, done(m))
                act.activation(ghi[:, 1:3, :], ps_t[:, 0:2 * N], ACT.Copy)
                act.activation(ghi[:, 0, :], ps_t[:, N:2 * N], ACT.Copy, scale=-1.0)\
                   .then_inc(gh_sb, 1)

            def sample(n, front, back):
                m = n + 1 if back else n
                if back:
                    act.wait_ge(back_sb, done(n))

                def step(s, g, k):
                    b, f, slot = n * S + s, m * S + s, k % 2
                    first, last = is_strip(s, 0), is_strip(s, S - 1)
                    if back:
                        act.wait_ge(x0_in[slot], uses(n, g, k) * 64)
                        act.wait_ge(c0_ps, before(b))
                        if first or last:
                            for p in range(2):
                                v = 1 if first and p == 0 else 2 if last and p == 1 else 0
                                op = act.activation(x0[:, p, 1:N + 1], x0raw[slot][:, p, :],
                                                    ACT.Identity, bias=cur_rb[:, v, 1:2],
                                                    scale=cur_rb[:, v, 0:1])
                        else:
                            op = act.activation(x0[:, :, 1:N + 1], x0raw[slot], ACT.Identity,
                                                bias=cur_rb[:, 0, 1:2], scale=cur_rb[:, 0, 0:1])
                        op.then_inc(x0_sb, 1)
                    if front:
                        act.wait_ge(t_ps, done(f))
                        act.wait_ge(y_ps, before(f))
                        act.activation(thi[:, :, :], ps_t[:, 0:2 * N], ACT.Copy).then_inc(th_sb, 1)
                    if back:
                        act.wait_ge(mix_ps, done(b))
                        act.wait_ge(sum_sb, before(b))
                        act.activation(sq[G:2 * G, 0, :], ps_mix[0:G, :], ACT.Square)
                        act.activation(sq[G:2 * G, 1, :], ps_mix[G:2 * G, :], ACT.Square)\
                           .then_inc(sq_sb, 1)
                    if front:
                        act.wait_ge(y_ps, done(f))
                        act.wait_ge(y_out, before(f, 16))
                        act.activation(ysb, ps_y[:, 0:2 * N], ACT.Copy).then_inc(y_sb, 1)
                    if back:
                        act.wait_ge(sum_sb, done(b))
                        act.wait_ge(lo_sb, before(b))
                        act.activation(mixed[G:2 * G], sq[G:2 * G, 0, :], ACT.Sqrt)\
                           .then_inc(abs_sb, 1)
                        act.wait_ge(c0_sb, done(b))
                        act.wait_ge(fft_sb, done(b))
                        act.wait_ge(abs_sb, done(b))
                        for v in range(2):
                            op = act.activation(rows(0, C, v, k), strip(mixed[0:C]), ACT.Copy)
                        op.then_inc(hi_sb, 1)
                        act.wait_ge(lo_sb, done(b))
                        src = ring32[0:G, 2, k * ROWS + 1:k * ROWS + 1 + ROWS, :]
                        act.activation(ring[2 * G:3 * G, 2, k * ROWS + 1:k * ROWS + 1 + ROWS, 0:N - 1],
                                       src[:, :, 2:N + 1], ACT.Copy)
                        act.activation(ring[3 * G:4 * G, 2, k * ROWS:k * ROWS + ROWS, 1:N + 1],
                                       src[:, :, 1:N + 1], ACT.Copy).then_inc(shift_sb, 1)
                strips(act, step)

            copy_g(0)
            sample(0, True, False)
            copy_g(1)
            with act.Fori(0, NS - 1) as n:
                sample(n, True, True)
                copy_g(n + 2)
            sample(NS - 1, False, True)

        @block.gpsimd
        def _(pool):
            pool.memset(ring32, 0.0).then_inc(border, 1)
            pool.wait_ge(credited, 1)

            def sample(n, front, back):
                m = n + 1 if back else n

                def step(s, g, k):
                    slot = k % 2
                    if front:
                        f = m * S + s
                        pool.wait_ge(raw_in[slot], uses(m, g, k) * 16)
                        pool.wait_ge(t_ps, before(f))
                        pool.wait_ge(xs_sb, before(f))
                        if back:
                            pool.wait_ge(sum_sb, before(n * S + s))
                        pool.sem_inc(turns, 1)
                        pool.tensor_copy(xhi[:, :], raw[slot][:, 0, :]).then_inc(xh_sb, 1)
                        pool.wait_ge(xh_sb, done(f))
                        pool.tensor_tensor(xlo[:, :], raw[slot][:, 0, :], xhi[:, :].bitcast(F32),
                                           ALU.subtract).then_inc(xs_sb, 1)
                    if back:
                        b = n * S + s
                        pool.wait_ge(sq_sb, done(b))
                        pool.wait_ge(abs_sb, before(b))
                        if front:
                            pool.wait_ge(xs_sb, done(m * S + s))
                        pool.wait_ge(sum_sb, before(b))
                        pool.tensor_tensor(sq[G:2 * G, 0, :], sq[G:2 * G, 0, :], sq[G:2 * G, 1, :],
                                           ALU.add).then_inc(sum_sb, 1)
                strips(pool, step)

            sample(0, True, False)
            with pool.Fori(0, NS - 1) as n:
                sample(n, True, True)
            sample(NS - 1, False, True)

        @block.vector
        def _(dve):
            tt, ts, stt, cp = dve.tensor_tensor, dve.tensor_scalar, dve.scalar_tensor_tensor, dve.tensor_copy
            linked = [0]

            def link(op):
                linked[0] += 1
                op.then_inc(dve_link, 1)
                dve.wait_ge(dve_link, linked[0])

            for k in range(2):
                dve.sem_inc(chunk_used, 1)
            with dve.Fori(0, NS) as n:
                for k in range(NCH):
                    dve.wait_ge(chunk_in[k % 2], (n * (NCH // 2) + (k // 2 + 1)) * 16)
                    for j in range(PER):
                        op = dve.bn_stats(stats[:, k * PER + j, :],
                                          chunk[k % 2][0:C, j * PIECE:(j + 1) * PIECE])
                    op.then_inc(chunk_used, 1)
                dve.wait_ge(chunk_used, (n + 1) * NCH + 2)
                dve.sem_inc(turns, 1)
                dve.bn_aggr(mv1[:, :], stats[:, :, :]).then_inc(stats_of, 1)
                dve.wait_ge(stats_of, n + 1)
                cp(mv[:, n, :], mv1[:, :]).then_inc(stats_kept, 1)
                dve.wait_ge(stats_kept, n + 1)
            dve.sem_inc(stats_end, 1)
            dve.memset(ones, 1.0).then_inc(ones_sb, 1)
            dve.wait_ge(setup_in, 16 * len(set_loads))
            dve.wait_ge(consts_in, 16 * len(loads))
            dve.sem_inc(mv_sb, 1)

            dve.wait_ge(mean_ps, 1)
            link(cp(msum[0:C], banks[0][0:C, 0:NS]))
            link(tt(dev[0:C], mv[:, :, 0], msum[0:C], ALU.subtract))
            link(tt(vdev[0:C], dev[0:C], dev[0:C], ALU.mult))
            tt(vdev[0:C], vdev[0:C], mv[:, :, 1], ALU.add).then_inc(vdev_sb, 1)
            dve.wait_ge(var_ps, 1)
            ts(vdev[0:C], banks[1][0:C, 0:NS], EPS, None, ALU.add).then_inc(veps_sb, 1)
            dve.wait_ge(sd_sb, 1)
            link(dve.reciprocal(t96[0:C, 0, :], vdev[0:C]))
            link(stt(t96[0:C, 1, :], msum[0:C], -1.0, t96[0:C, 0, :], ALU.mult, ALU.mult))
            tt(gap[0:C], dev[0:C], t96[0:C, 0, :], ALU.mult).then_inc(gap_sb, 1)
            dve.wait_ge(l1_ps, 1)
            link(cp(cst, banks[2][:, 0:6 * NS].rearrange("p (a b c) -> p a b c", a=3, b=2)))
            link(cp(rb0[:, :, :], cst[:, 0].rearrange("p a b -> p b a")))
            dve.wait_ge(l2_ps, 1)
            cp(gi, banks[4][:, 0:6 * NS].rearrange("p (a b) -> p a b", a=6)).then_inc(gi_sb, 1)
            dve.wait_ge(gi_sb, 1)

            def per_sample(a, width):
                return a[:, :, None].to_broadcast([a.shape[0], a.shape[1], width])

            dve.wait_ge(hid_sb, 1)
            for k, f in enumerate(WIDTH):
                if k:
                    dve.wait_ge(go_ps, k)
                tt(hidw[0:9, :, 0:f], per_sample(hid[0:9, k + 1, :], f),
                   mlpgo[0:9, None, k * 2 * G:k * 2 * G + f].to_broadcast([9, NS, f]),
                   ALU.mult).then_inc(hidw_sb, 1)
                dve.wait_ge(go_ps, k + 1)
                for v in range(2 if k < 2 else 1):
                    for j in range(NFC):
                        op = tt(gate[v][:, j * FC:(j + 1) * FC, 0:f],
                                banks[GOBANK[k] + j][:, 0:FC * f].rearrange("p (a b) -> p a b", b=f),
                                per_sample(gi[:, 1 + 2 * k + v, j * FC:(j + 1) * FC], f), ALU.mult)
                op.then_inc(logit_sb, 1)
                dve.wait_ge(gate_sb, k + 1)
                if k == 2:
                    link(cp(gate0[:, :, :], gate[0][:, :, 0:G]))
                    continue
                wl = (w05l, w1l)[k]
                for v in range(2):
                    link(stt(gate[v], gate[v], 0.5,
                             wl[:, None, v, :].to_broadcast([N, NS, 2 * G]), ALU.mult, ALU.mult))
                lo, hi = slice(0, G), slice(G, 2 * G)
                A, Cw, B, D = gate[0][:, :, lo], gate[0][:, :, hi], gate[1][:, :, lo], gate[1][:, :, hi]
                g = [slice(q * G, (q + 1) * G) for q in range(4)]
                if k == 0:
                    tt(w_freq[g[0], :, lo], A[g[0]], D[g[0]], ALU.add)
                    tt(w_freq[g[0], :, hi], Cw[g[0]], B[g[0]], ALU.subtract)
                    tt(w_freq[g[1], :, lo], A[g[1]], D[g[1]], ALU.subtract)
                    tt(w_freq[g[1], :, hi], B[g[1]], Cw[g[1]], ALU.add)
                    stt(w_freq[g[2], :, lo], B[g[2]], -1.0, Cw[g[2]], ALU.mult, ALU.subtract)
                    link(tt(w_freq[g[2], :, hi], A[g[2]], D[g[2]], ALU.subtract))
                else:
                    tt(w_fft[g[0], :, :], A[g[0]], D[g[0]], ALU.add)
                    tt(w_fft[g[1], :, :], B[g[1]], Cw[g[1]], ALU.subtract)
                    tt(w_fft[g[2], :, :], A[g[2]], D[g[2]], ALU.subtract)
                    link(tt(w_fft[g[3], :, :], B[g[3]], Cw[g[3]], ALU.add))

            link(dve.memset(bsel, 0.0))
            link(dve.memset(bmir, 0.0))
            bcol = cst[:, 1, 1, :]
            cp(bsel[G:2 * G, :, 0], bcol[G:2 * G])
            cp(bsel[2 * G:3 * G, :, 1], bcol[2 * G:3 * G])
            cp(bsel[0:G, :, 4], bcol[0:G])
            cp(bmir[0:G], cst[0:G, 2, 1, :])
            cp(bmir[2 * G:3 * G], cst[2 * G:3 * G, 2, 1, :]).then_inc(mixw_sb, 1)
            link(tt(brow[C:N], b05rows[C:N], sgn[C:N], ALU.mult))
            dve.wait_ge(sums_ps, 1)
            for j in range(NFC):
                tt(w_freq[C:C + NP, j * FC:(j + 1) * FC, :],
                   banks[j][C:C + NP, 0:FC * 2 * G].rearrange("p (a b) -> p a b", b=2 * G),
                   brow[C:C + NP, None, :].to_broadcast([NP, FC, 2 * G]), ALU.add)
            cp(bias_fft[2 * G:3 * G, :], banks[7][2 * G:3 * G, 0:NS])
            tt(w_freq[0:C], w_freq[0:C], per_sample(cst[0:C, 1, 0, :], 2 * G), ALU.mult)
            link(tt(w_fft[:, :, :], w_fft[:, :, :], per_sample(cst[:, 2, 0, :], G), ALU.mult))

            dve.wait_ge(alpha_sb, 1)
            link(ts(alpha, alpha, 0.8, 0.1, ALU.mult, ALU.add))
            for k in range(4):
                link(ts(turn[:, k, :], alpha, cols[:, k:k + 1], (0.25, 0.0)[k % 2],
                        ALU.mult, ALU.add))
            link(ts(whole, turn, ROUND, None, ALU.add))
            link(ts(whole, whole, ROUND, None, ALU.subtract))
            tt(turn, turn, whole, ALU.subtract).then_inc(turn_sb, 1)
            dve.wait_ge(trig_sb, 1)
            link(dve.memset(tab[:, :, :], 0.0))
            for k in range(2):
                for j in range(4):
                    c = trig[:, 2 * k + j % 2, :]
                    link(ts(tab[:, 0:NS, 4 * k + j], c, cols[:, 4 + k:5 + k],
                            -1.0 if j == 3 else 1.0, ALU.mult, ALU.mult))
            for j in range(2):
                link(cp(tab[:, 0:NS, 8 + j], trig[:, j, :]))
            dve.wait_ge(w2hi_sb, 1)
            link(tt(w2b[0:C, :, :], w2raw[0:C], w2a[0:C, :, :].bitcast(F32), ALU.subtract))
            dve.wait_ge(ones_out, 32)
            link(dve.memset(x0, 0.0))
            link(dve.memset(x0raw[0], 0.0))
            dve.wait_ge(border, 1)
            for s_, v in credits:
                dve.sem_inc(s_, v)
            dve.sem_inc(credited, 1)

            def table(m):
                dve.wait_ge(row_ps, before(m))
                cp(cur_tab[:, :], tab[:, m, :]).then_inc(tab_sb, 1)
                dve.wait_ge(tab_sb, done(m))
                dve.wait_ge(g_ps, before(m))
                for j in range(2):
                    op = ts(el[:, j, :], ET, cur_tab[:, 8 + j:9 + j], None, ALU.mult)
                op.then_inc(el_sb, 1)

            def plane_rows(m):
                dve.wait_ge(row_ps, done(m))
                dve.wait_ge(pl_ps, before(m))
                for k, bank in enumerate((ps_y, ps_h)):
                    op = cp(prow[:, k].rearrange("p a b -> p (a b)"), bank[0:2, 0:3 * N])
                op.then_inc(row_sb, 1)

            def planes(m):
                dve.wait_ge(pl_ps, done(m))
                dve.wait_ge(pl_out, before(m, 16))
                cp(pimg[:, :, :].rearrange("p a b -> p (a b)"), ps_ht[:, :]).then_inc(pl_sb, 1)

            def weights(n):
                dve.wait_ge(c0_ps, before(n * S))
                dve.wait_ge(mix_ps, before(n * S))
                dve.wait_ge(x0_sb, before(n * S))
                dve.wait_ge(fft_sb, before(n * S))
                cp(cur_freq[0:C + NP, :], w_freq[0:C + NP, n, :])
                cp(cur_fft[:, :], w_fft[:, n, :])
                cp(cur_bf[2 * G:3 * G, :], bias_fft[2 * G:3 * G, bass.ds(n, 1)])
                cp(cur_rb[:, 0, :], rb0[:, n, :])
                for k in range(2):
                    ts(cur_rb[:, 1 + k, :], rb0[:, n, :], cols[:, 6 + k:7 + k], None, ALU.mult)
                for dw in range(3):
                    op = tt(cur_w0[:, dw], w0l[:, dw],
                            gate0[:, n, None, :].to_broadcast([N, 2, G]), ALU.mult)
                op.then_inc(back_sb, 1)

            def low_g(m):
                dve.wait_ge(gh_sb, done(m))
                tt(glo[:, 1:3, :], ps_t[:, 0:2 * N].rearrange("p (a b) -> p a b", a=2),
                   ghi[:, 1:3, :].bitcast(F32), ALU.subtract)
                stt(glo[:, 0, :], ps_t[:, N:2 * N], -1.0, ghi[:, 0, :].bitcast(F32),
                    ALU.mult, ALU.subtract).then_inc(gl_sb, 1)

            def last_conv(b, slot, filled):
                dve.wait_ge(c2_ps, done(b))
                dve.wait_ge(res_in[slot], filled * 16)
                dve.wait_ge(px_out, before(b, 16))
                stt(ost[0:C], ps_c2[slot][0:C, :], b2c[:, 0:1], xres[slot][0:C],
                    ALU.add, ALU.add).then_inc(px_sb, 1)

            def sample(n, front, back, prepare):
                m = n + 1 if back else n

                def step(s, g, k):
                    b, f, slot = n * S + s, m * S + s, k % 2
                    if front:
                        dve.wait_ge(ht_ps, done(f))
                        dve.wait_ge(h_ps, before(f))
                        cp(htsb.rearrange("p a b -> p (a b)"), ps_ht[:, 0:2 * N]).then_inc(ht_sb, 1)
                        dve.wait_ge(th_sb, done(f))
                        tt(tlo[:, :, :], ps_t[:, 0:2 * N].rearrange("p (a b) -> p a b", a=2),
                           thi[:, :, :].bitcast(F32), ALU.subtract).then_inc(tl_sb, 1)
                    if back:
                        dve.wait_ge(c0_ps, done(b))
                        dve.wait_ge(hi_sb, before(b))
                        dve.wait_ge(lo_sb, before(b))
                        for q in range(ROWS):
                            p = slice(q * G, (q + 1) * G)
                            op = ts(mixed[0:G, q * N:(q + 1) * N], ps_c0[p, 0:N], b0c[p, 0:1], None,
                                    ALU.add)
                        op.then_inc(c0_sb, 1)
                        dve.wait_ge(mix_ps, done(b))
                        ts(mixed[2 * G:3 * G], ps_mix[2 * G:3 * G, :], cur_bf[2 * G:3 * G, 0:1], None,
                           ALU.add).then_inc(fft_sb, 1)
                    if front:
                        dve.wait_ge(h_ps, done(f))
                        dve.wait_ge(h_out, before(f, 16))
                        cp(hsb.rearrange("p a b -> p (a b)"), ps_h[:, 0:3 * N]).then_inc(h_sb, 1)
                    if back:
                        dve.wait_ge(hi_sb, done(b))
                        for q, (p0, which) in enumerate(((3 * G, 0), (3 * G, 1), (0, 2))):
                            p = slice(q * G, (q + 1) * G)
                            tt(rows(p0, p0 + G, which, k), strip(mixed[p]),
                               rows(q * G, (q + 1) * G, 0, k).bitcast(F32), ALU.subtract)
                        p = slice(2 * G, 3 * G)
                        tt(ring[G:2 * G, 2, k * ROWS + 1:k * ROWS + 1 + ROWS, 0:N], strip(mixed[p]),
                           rows(2 * G, 3 * G, 0, k).bitcast(F32), ALU.subtract).then_inc(lo_sb, 1)
                    if is_strip(s, S - 1) and prepare:
                        table(m + 1)
                    if back and not (is_strip(s, 0) or is_strip(s, 1)):
                        last_conv(b - LAG, slot, uses(n, g, k) - 1)
                    if back:
                        if is_strip(s, 0):
                            dve.sem_inc(twin_sb, 1)
                        elif k == 0:
                            dve.wait_ge(shift_sb, done(b))
                            cp(ring[:, :, RING - 1, :], ring32[:, :, 1, :]).then_inc(twin_sb, 1)
                        elif is_strip(s, S - 1):
                            dve.wait_ge(shift_sb, done(b))
                            dve.memset(ring32[:, :, 0:RING:RING - 1, :], 0.0).then_inc(border_sb, 1)
                        elif k == GROUP - 1:
                            dve.wait_ge(shift_sb, done(b))
                            cp(ring[:, :, 0, :], ring32[:, :, RING - 2, :])
                strips(dve, step)
                if back and prepare:
                    weights(n + 1)
                for s in range(S - LAG, S):
                    if back:
                        last_conv(n * S + s, s % 2, (n + 1) * (S // 2))
                    if s == S - LAG and prepare and back:
                        plane_rows(m + 1)
                if back and prepare:
                    low_g(m + 1)
                    planes(m + 1)

            table(0)
            plane_rows(0)
            low_g(0)
            planes(0)
            sample(0, True, False, True)
            weights(0)
            plane_rows(1)
            low_g(1)
            planes(1)
            with dve.Fori(0, NS - 1) as n:
                sample(n, True, True, True)
            sample(NS - 1, False, True, False)


def lay_out(inputs):
    w = {k.replace("L0_conv_", ""): np.asarray(v) for k, v in inputs.items() if k != "x"}
    f32 = np.float32
    p = np.arange(N) % G

    def gated(conv):
        t = conv[:, :, 0, 0]
        return np.stack([t[:, v * G + p].T for v in range(2)], axis=1)

    w0l = np.zeros((4, G, 3, 2, G), f32)
    for r in range(4):
        for q in range(2):
            if 0 <= r - q <= 2:
                w0l[r, :, :, q, :] = w["conv0_w"][:, :, r - q, :].transpose(1, 2, 0)
    mlp1 = np.zeros((C, 4, 9), f32)
    mlp1b = np.ones((9, 4), f32)
    for k, (name, at) in enumerate((("alpha", G), ("gfreq", G), ("gfft", 2 * G), ("gsp", 0))):
        mlp1[at:at + G, k, 0:8] = w[name + "_w1"].T
        mlp1b[0:8, k] = w[name + "_b1"]

    def second(name, feature):
        return np.concatenate([w[name + "_w2"][feature].T, w[name + "_b2"][None, feature]])

    mlp2 = np.stack([second("alpha", 0 * p), second("gfreq", 2 * G + p), second("gfreq", 3 * G + p),
                     second("gfft", 2 * G + p), second("gfft", 3 * G + p), second("gsp", G + p)],
                    axis=1)
    mlpgo = np.concatenate([second("gfreq", np.arange(2 * G)), second("gfft", np.arange(2 * G)),
                            second("gsp", np.arange(G))], axis=1)
    w2l = w["conv2_w"].transpose(1, 2, 3, 0).reshape(C, 9, C)
    w2c = np.zeros((4, G, len(CORNERS), C), f32)
    for j, ((row, col), groups) in enumerate(CORNERS):
        for q in groups:
            w2c[q, :, j, :] = w2l[2 * G:, 3 * (row + SHIFTS[q][0]) + col + SHIFTS[q][1], :]
    b05rows = np.zeros((N, 2 * G), f32)
    b05rows[98] = w["conv05_b"]
    b05rows[99, 0:G] = w["conv05_b"][G:]
    b05rows[99, G:] = w["conv05_b"][:G]
    return {
        "w0l": w0l.reshape(N, 3, 2, G), "w2a": np.concatenate([w2l, w2l[0:G]]), "w2b": w2l[G:2 * G],
        "w2c": w2c.reshape(N, len(CORNERS), C),
        "b0c": w["conv0_b"][p][:, None], "b2c": w["conv2_b"][:, None],
        "b1rows": w["conv1_b"].reshape(2, G), "w05l": gated(w["conv05_w"]),
        "w1l": gated(w["conv1_w"]), "b05rows": b05rows, "mlp1": mlp1, "mlp1b": mlp1b,
        "mlp2": mlp2, "mlpgo": mlpgo,
    }


def kernel(**inputs):
    import concourse.bacc as bacc
    from concourse.bass_utils import run_bass_kernel_spmd

    nc = bacc.Bacc("TRN2", target_bir_lowering=False, num_devices=1)
    x = np.ascontiguousarray(inputs["x"])
    arrays = {"x": x}
    arrays.update(constants())
    arrays.update({k: np.ascontiguousarray(v) for k, v in lay_out(inputs).items()})
    aps = {k: nc.dram_tensor("in_" + k, a.shape, mybir.dt.from_np(a.dtype), kind="ExternalInput").ap()
           for k, a in arrays.items()}
    out = nc.dram_tensor("out", x.shape, mybir.dt.from_np(x.dtype), kind="ExternalOutput").ap()
    build(nc, aps.pop("x"), out, aps)
    arrays = {"in_" + k: a for k, a in arrays.items()}
    r = run_bass_kernel_spmd(nc, [arrays], core_ids=[0])
    return r.results[0]["out"]
```

```python
from contextlib import ExitStack

import numpy as np

import concourse.bass as bass
from concourse import mybir

F32 = mybir.dt.float32
F32R = mybir.dt.float32r
ALU = mybir.AluOpType
ACT = mybir.ActivationFunctionType

N = 128
C = 96
G = C // 3
ROWS = 4
S = N // ROWS
PX = ROWS * N
HW = N * N
NP = 5
EPS = 1e-5
TWO_PI = 6.283185
ROUND = 12582912.0
PIECE = 512
THIRDS = C * HW // N // (8 * PIECE)
PIECES = 8 * THIRDS
LAG = 2
UNITS = 9
BLOCKS = ("alpha", "gfreq", "gfreq", "gfft", "gfft", "gsp")
NH = UNITS * len(BLOCKS)
GROUP = 4
RING = GROUP * ROWS + 2
SHIFTS = ((0, 0), (0, 1), (0, 2), (1, 0))
CORNERS = (((0, 0), (0, 1, 2, 3)), ((2, 0), (0, 1, 2)), ((1, 1), (0, 1)))
STATS_GROUPS = PIECES // GROUP
assert S == G and S % GROUP == 0 and THIRDS == 3 and STATS_GROUPS == 6


def eigenvectors():
    import math
    s = np.zeros(N, dtype=np.float64)
    s[1] = 1.0
    s[N - 1] = 1.0
    idx = (np.arange(N)[:, None] - np.arange(N)[None, :]) % N
    shifted = s[idx] + np.diag(np.fft.fft(s).real)
    r = N // 2
    even = 1 - N % 2
    P = np.zeros((N, N))
    P[0, 0] = 1.0
    for i in range(1, r - even + 1):
        P[i, i] = 1 / math.sqrt(2)
        P[i, N - i] = 1 / math.sqrt(2)
    if even:
        P[r, r] = 1.0
    for i in range(r + 1, N):
        P[i, i] = -1 / math.sqrt(2)
        P[i, N - i] = 1 / math.sqrt(2)
    CS = P @ shifted @ P.T
    h = N // 2 + 1
    ec, vc = np.linalg.eigh(CS[:h, :h])
    es, vs = np.linalg.eigh(CS[h:, h:])
    vc = vc[:, np.argsort(-ec)]
    vs = vs[:, np.argsort(-es)]
    SC2 = P @ np.vstack([vc, np.zeros((N - h, h))])
    SS2 = P @ np.vstack([np.zeros((h, N - h)), vs])
    E = np.zeros((N, N + 1))
    SS2 = np.hstack([SS2, np.zeros((N, 1))])
    E[:, 0:N + 1:2] = SC2
    E[:, 1:N:2] = SS2
    return np.delete(E, N - 1, axis=1).astype(np.float32)


def constants():
    f32 = np.float32
    E = eigenvectors().astype(np.float64)
    n = np.arange(N)
    odd = n % 2 == 1
    hil = np.where(odd, 2 / N / np.tan(np.pi * np.where(odd, n, 1) / N), 0.0)
    HT = hil[(n[None, :] - n[:, None]) % N]
    neg = (-n) % N
    flip = np.eye(N)[neg]
    mats = np.stack([np.roll(E, N // 2, axis=1), np.eye(N), HT, flip, HT[:, neg]], axis=1)
    power = np.concatenate([np.arange(N - 1), [N]])
    ones = E.sum(1)
    cols = np.zeros((N, 28))
    cols[:, 0] = cols[:, 1] = power / 2
    cols[:, 2] = cols[:, 3] = power / 4
    cols[:, [8, 10]] = 0.25
    cols[:, 12:16] = ones[:, None] * [1, 1, 1, -1]
    cols[:, 16:20] = ones[:, None] / np.sqrt(N) * [1, 1, 1, -1]
    cols[G:2 * G, 20] = cols[2 * G:C, 21] = cols[0:G, 24] = 1
    cols[0:G, 25] = cols[2 * G:C, 25] = 1
    cols[:, 6] = np.where(n < G, 0, 1)
    cols[:, 7] = np.where(n < 3 * G, 1, 0)
    sel = np.zeros((C, 3, N))
    for k, src in enumerate((0, G, 2 * G)):
        sel[src + n % G, k, n] = 1
    quarter = (3 * n[:, None] + np.arange(3)) // 4
    c = np.arange(C)
    same_group = n[:, None] // 4 == c // 3
    means = np.zeros((N, N + 4 * C))
    means[:, 0:N] = (n[:, None] // 4 == n // 4) / 12
    means[:, N:N + C] = same_group / 12
    means[:, N + C:] = (quarter[:, :, None] == c).reshape(N, 3 * C) / 4
    sgn = np.zeros((N, 2 * G))
    sgn[98] = 1
    sgn[99, :G] = -1
    sgn[99, G:] = 1
    own = np.kron(np.eye(len(BLOCKS)), np.ones((UNITS, 1)))
    row0 = np.stack([np.eye(N)[0], -hil])
    return {"c_mats": mats.astype(f32), "c_cols": cols.astype(f32), "c_sel": sel.astype(f32),
            "c_means": means.astype(f32), "c_own": own.astype(f32), "c_sgn": sgn.astype(f32),
            "c_row0": row0.astype(f32)}


def build(nc, x, out, cs):
    NS = x.shape[0]
    x_rows = x.rearrange("n c h w -> n c (h w)")
    x_stat = x.rearrange("n c h w -> n (c h w)").rearrange("n (p f) -> n p f", p=N)
    x_img = x[:, G:C].rearrange("n (t c) h w -> n t h c w", t=2)
    x_mix = x_rows[:, G:C].rearrange("n (t c) f -> n c t f", t=2)
    out_rows = out.rearrange("n c h w -> n c (h w)")
    scr = nc.dram_tensor("planes", (2, 5 * G, HW), F32, kind="Internal").ap()
    scr_img = scr.rearrange("b (t c) (h w) -> b c h t w", t=5, w=N)
    scr_k = nc.dram_tensor("constant_planes", (2, NP, HW), F32, kind="Internal").ap()
    scr_k_img = scr_k.rearrange("b k (h w) -> b h k w", w=N)

    with ExitStack() as ctx:
        def sb(name, shape, dt=F32):
            return ctx.enter_context(nc.sbuf_tensor(name, shape, dt))

        def sem(name):
            return ctx.enter_context(nc.semaphore(name))

        mats = sb("mats", [N, 5, N])
        ET, EYE, HT, FLIP = (mats[:, k, :] for k in range(4))
        cols = sb("cols", [N, 28])
        w0l = sb("w0l", [N, 3, 2, G])
        w2a = sb("w2a", [N, 9, C], F32R)
        w2b = sb("w2b", [N, 9, C], F32R)
        w2c = sb("w2c", [N, len(CORNERS), C], F32R)
        b0c = sb("b0c", [N, 1])
        b2c = sb("b2c", [C, 1])
        b1rows = sb("b1rows", [2, G])
        row0 = sb("row0", [2, N])
        ring = sb("ring", [N, 3, RING, N + 2], F32R)
        ring32 = ring[:, :, :, :].bitcast(F32)
        stat_raw = [sb(f"stat_raw{i}", [N, 2 * PIECE]) for i in range(2)]
        stats = sb("stats", [N, PIECES, 6])
        mv = sb("mv", [N, THIRDS, 2])
        w_mix = sb("w_mix", [N, 4, 2 * G])
        sel, means = sb("sel", [C, 3, N]), sb("means", [N, N + 4 * C])
        sgn, b05rows, brow = sb("sgn", [N, 2 * G]), sb("b05rows", [N, 2 * G]), sb("brow", [N, 2 * G])
        mlp1, mlp1b = sb("mlp1", [C, NH]), sb("mlp1b", [NH, 1])
        mlp2, mlpgo = sb("mlp2", [NH, N]), sb("mlpgo", [NH, 5 * G])
        own = sb("own", [NH, len(BLOCKS)])
        ones = sb("ones", [N, N])
        gm, chm, dev, ssq = sb("gm", [N, 1]), sb("chm", [C, 2]), sb("dev", [N, 3]), sb("ssq", [N, 3])
        sd, t96, gap = sb("sd", [C, 1]), sb("t96", [C, 2]), sb("gap", [C, 1])
        hid, hidb, hidw = sb("hid", [NH, 1]), sb("hidb", [NH, len(BLOCKS)]), sb("hidw", [NH, 5 * G])
        mean3 = sb("mean3", [N, 1])
        cst = sb("cst", [N, 3, 2])
        gi = sb("gi", [N, 6])
        gates = sb("gates", [N, 9 * G + 1])
        angle, turn, whole, trig = (sb(nm, [N, w]) for nm, w in
                                    (("angle", 1), ("turn", 4), ("whole", 4), ("trig", 4)))
        bsel, bmir = sb("bsel", [N, NP]), sb("bmir", [N, 1])
        new_freq, new_fft = sb("new_freq", [N, 2 * G]), sb("new_fft", [N, G])
        new_bias = sb("new_bias", [N, 1])
        next_freq, next_fft = sb("next_freq", [N, 2 * G]), sb("next_fft", [N, G])
        next_bias, next_rb, next_w0 = sb("next_bias", [N, 1]), sb("next_rb", [N, 2]), sb("next_w0", [N, G])
        cur_tab = sb("cur_tab", [N, 10])
        cur_rb = sb("cur_rb", [N, 3, 2])
        cur_bf = sb("cur_bf", [N, 1])
        cur_freq = sb("cur_freq", [N, 2 * G])
        cur_fft = sb("cur_fft", [N, G])
        cur_w0 = sb("cur_w0", [N, 3, 2, G])
        el = sb("el", [N, 2, N])
        ghi = sb("ghi", [N, 3, N], F32R)
        glo = sb("glo", [N, 3, N], F32R)
        xhi, xlo = sb("xhi", [N, N], F32R), sb("xlo", [N, N], F32R)
        thi, tlo = sb("thi", [N, 2, N], F32R), sb("tlo", [N, 2, N], F32R)
        prow = sb("prow", [2, 2, 3, N])
        pimg = sb("pimg", [N, 4, N])
        arena = sb("arena", [N, 14000])
        at = [0]

        def carve(*dims):
            size = int(np.prod(dims))
            a = arena[:, at[0]:at[0] + size]
            at[0] += size
            assert at[0] <= 14000
            names = " ".join("abc"[:len(dims)])
            if len(dims) == 1:
                return a
            sizes = {k: d for k, d in zip("abc", dims)}
            return a.rearrange(f"p ({names}) -> p {names}", **sizes)

        w2raw, w2braw = carve(9, C), carve(9, C)
        w2craw = carve(len(CORNERS), C)
        at[0] = 0
        raw = [carve(2, 2, N) for _ in range(2)]
        mixin = [carve(2, 2 * PX) for _ in range(2)]
        x0raw = [carve(4, N) for _ in range(2)]
        xres = [carve(2 * PX) for _ in range(2)]
        ost = [carve(2 * PX) for _ in range(2)]
        x0 = carve(2, N + 2)
        htsb = carve(2, N)
        planes_sb = [carve(5, N) for _ in range(2)]
        sq = carve(2, PX)
        mixed = carve(PX)
        table_load = sb("table_load", [1, 1])

        banks = [ctx.enter_context(nc.psum_tensor(f"bank{i}", [N, 512], F32)) for i in range(8)]
        ps_c2 = banks[0:2]
        ps_mix, ps_c0, ps_t, ps_y, ps_ht, ps_h = banks[2:8]

        col = {}
        at[0] = 0
        for name, width in (("gm", 1), ("chm", 1), ("gmc", 1), ("var", 1), ("cst", 6), ("l1", 1),
                            ("l2", 6), ("go", 5 * G), ("sums", 2 * G), ("bias", 1)):
            col[name] = slice(at[0], at[0] + width)
            at[0] += width
        assert at[0] <= 512

        def free_bank(k):
            return ps_c2[(k + 1) % 2]

        MEANS, VARIANCES, LAYERS, SIGMOIDS, SINES, SUMS = (PIECES + j for j in range(6))

        consts_in = sem("consts_in")
        setup_in, brow_sb = sem("setup_in"), sem("brow_sb")
        stat_in = [sem(f"stat_in{i}") for i in range(2)]
        piece_sb, link_sb, start_link = sem("piece_sb"), sem("link_sb"), sem("start_link")
        ones_sb, mv_sb, dev_sb, veps_sb = sem("ones_sb"), sem("mv_sb"), sem("dev_sb"), sem("veps_sb")
        mean_ps, var_ps, sd_sb, gap_sb = sem("mean_ps"), sem("var_ps"), sem("sd_sb"), sem("gap_sb")
        l1_ps, hidw_sb, go_ps = sem("l1_ps"), sem("hidw_sb"), sem("go_ps")
        logit_sb, gate_sb, turn_sb, trig_sb = sem("logit_sb"), sem("gate_sb"), sem("turn_sb"), sem("trig_sb")
        mixw_sb, sums_ps, new_sb, next_sb = sem("mixw_sb"), sem("sums_ps"), sem("new_sb"), sem("next_sb")
        w2hi_sb = sem("w2hi_sb")
        ones_out = sem("ones_out")
        border = sem("border")

        raw_in = [sem(f"raw_in{i}") for i in range(2)]
        mix_in = [sem(f"mix_in{i}") for i in range(2)]
        planes_in = [sem(f"planes_in{i}") for i in range(2)]
        x0_in = [sem(f"x0_in{i}") for i in range(2)]
        res_in = [sem(f"res_in{i}") for i in range(2)]
        ch_out = [sem(f"ch_out{i}") for i in range(2)]
        px_out = [sem(f"px_out{i}") for i in range(2)]
        pl_out = sem("pl_out")
        xs_sb, t_ps, th_sb, tl_sb = sem("xs_sb"), sem("t_ps"), sem("th_sb"), sem("tl_sb")
        xh_sb = sem("xh_sb")
        ht_ps, ht_sb = sem("ht_ps"), sem("ht_sb")
        y_ps, y_sb = sem("y_ps"), sem("y_sb")
        h_ps, h_sb = sem("h_ps"), sem("h_sb")
        x0_sb, c0_ps, c0_sb = sem("x0_sb"), sem("c0_ps"), sem("c0_sb")
        mix_ps, sq_sb, sum_sb = sem("mix_ps"), sem("sq_sb"), sem("sum_sb")
        abs_sb, fft_sb = sem("abs_sb"), sem("fft_sb")
        hi_sb, lo_sb, shift_sb = sem("hi_sb"), sem("lo_sb"), sem("shift_sb")
        lo2_sb = sem("lo2_sb")
        twin_sb, border_sb = sem("twin_sb"), sem("border_sb")
        c2_ps, px_sb = sem("c2_ps"), sem("px_sb")
        tab_sb, el_sb, g_ps = sem("tab_sb"), sem("el_sb"), sem("g_ps")
        gh_sb, gl_sb = sem("gh_sb"), sem("gl_sb")
        row_ps, row_sb, pl_ps, pl_sb = sem("row_ps"), sem("row_sb"), sem("pl_ps"), sem("pl_sb")
        back_sb = sem("back_sb")
        credited = sem("credited")
        turns = sem("turns")

        credits = [(s, 1) for s in (t_ps, th_sb, tl_sb, xs_sb, xh_sb, ht_ps, ht_sb, y_ps, y_sb,
                                    h_ps, h_sb, x0_sb, c0_ps, c0_sb, mix_ps, sq_sb, sum_sb, abs_sb,
                                    fft_sb, hi_sb, lo_sb, shift_sb, twin_sb, border_sb, lo2_sb,
                                    c2_ps, px_sb, tab_sb, el_sb, g_ps, gh_sb, gl_sb, row_ps, row_sb,
                                    pl_ps, pl_sb, back_sb)]
        credits += [(s, 16) for s in (pl_out, *ch_out, *px_out)]

        def done(item, per=1):
            return (item + 1) * per + per

        def before(item, per=1):
            return item * per + per

        def channel_use(image, g, k):
            return image * (S // 2) + (g * 2 + k // 2)

        def pixel_use(image, g):
            return image * (S // GROUP) + g

        def strips(eng, step):
            for k in range(GROUP):
                step(k, 0, k)
            with eng.Fori(1, STATS_GROUPS - 1) as g:
                for k in range(GROUP):
                    step(g * GROUP + k, g, k)
            for g in range(STATS_GROUPS - 1, S // GROUP):
                for k in range(GROUP):
                    step(g * GROUP + k, g, k)

        def s_half(g, k):
            return g * (GROUP // 2) + k // 2

        def is_strip(s, which):
            return isinstance(s, int) and s == which

        def slot_of(k):
            return k // 2

        def uses(image, g):
            return image * (S // GROUP) + (g + 1)

        loads = [(mats[:, :, :], cs["c_mats"]), (cols[:, :], cs["c_cols"]),
                 (w0l[:, :, :, :], cs["w0l"]), (b0c[:, :], cs["b0c"]), (b2c[:, :], cs["b2c"]),
                 (b1rows[:, :], cs["b1rows"]), (row0[:, :], cs["c_row0"])]
        set_loads = [(means[:, :], cs["c_means"]), (sel[:, :, :], cs["c_sel"]),
                     (mlp1[:, :], cs["mlp1"]), (mlp1b[:, :], cs["mlp1b"]),
                     (mlp2[:, :], cs["mlp2"]), (own[:, :], cs["c_own"]), (mlpgo[:, :], cs["mlpgo"]),
                     (w_mix[:, :, :], cs["w_mix"]), (sgn[:, :], cs["c_sgn"]),
                     (b05rows[:, :], cs["b05rows"]), (w2raw, cs["w2a"]),
                     (w2braw[C:N], cs["w2b"]), (w2craw, cs["w2c"])]

        def strip(a):
            return a.rearrange("p (r w) -> p r w", w=N)

        def rows(p0, p1, which, k):
            return ring[p0:p1, which, k * ROWS + 1:k * ROWS + 1 + ROWS, 1:N + 1]

        GATE_COLS = ((0, 2 * G), (2 * G, 4 * G), (4 * G, 5 * G))

        block = ctx.enter_context(nc.Block())

        @block.sync
        def _(sp):
            def load_stats(q, t, slot):
                sp.dma_start(stat_raw[slot][:, :], x_stat[q, :, bass.ds(t * 2 * PIECE, 2 * PIECE)])\
                  .then_inc(stat_in[slot], 16)

            small = [(d, c_, setup_in) for d, c_ in set_loads] + [(d, c_, consts_in) for d, c_ in loads]
            for t in range(PIECES // 2):
                if t >= 2:
                    sp.wait_ge(piece_sb, 2 * (t - 1))
                load_stats(0, t, t % 2)
                for dst, src, loaded in small[2 * t:2 * t + 2]:
                    sp.dma_start(dst, src).then_inc(loaded, 16)
            assert len(small) <= PIECES
            sp.wait_ge(ones_sb, 1)
            for par in range(2):
                sp.dma_start(scr_k_img[par, :, NP - 1, :], ones[:, :]).then_inc(ones_out, 16)
            sp.wait_ge(credited, 1)

            def load_raw(m, s, slot, first=False):
                if not first:
                    sp.wait_ge(t_ps, done(m * S + s - 3))
                    sp.wait_ge(ht_ps, done(m * S + s - 3))
                    sp.sem_inc(turns, 1)
                for t in range(2):
                    sp.dma_start(raw[slot][:, t], x_img[m, t, :, bass.ds(s, 2)])\
                      .then_inc(raw_in[slot], 16)

            def load_pixels(n, s, slot, first=False, last=False, now=None):
                if now is not None:
                    sp.wait_ge(x0_sb, done(now - 1))
                r0 = s * ROWS
                for r in range(4):
                    p0 = 1 if first and r == 0 else 0
                    p1 = 3 if last and r == 3 else 4
                    if p1 - p0 == 4:
                        odd = r // 2
                        src = x[n, 0:G, bass.ds(r0 + (r - 1 - odd), 8), :]\
                            .rearrange("c (p t) w -> c p t w", t=2)[:, :, odd, :]
                    else:
                        src = x[n, 0:G, bass.ds(r0 + (2 * p0 + r - 2), 6), :]\
                            .rearrange("c (p t) w -> c p t w", t=2)[:, :, 1, :]
                    sp.dma_start(x0raw[slot][r * G:(r + 1) * G, p0:p1, :], src)\
                      .then_inc(x0_in[slot], 16)
                if now is not None:
                    sp.wait_ge(mix_ps, done(now - 1))
                sp.dma_start(mixin[slot][0:G], x_mix[n, :, :, bass.ds(s * PX, 2 * PX)])\
                  .then_inc(mix_in[slot], 16)

            def load_planes(par, s, slot):
                px = bass.ds(s * PX, 2 * PX)
                sp.dma_start(mixin[slot][G:3 * G, 0], scr[par, 0:2 * G, px])\
                  .then_inc(planes_in[slot], 16)
                sp.dma_start(mixin[slot][G:4 * G, 1], scr[par, 2 * G:5 * G, px])\
                  .then_inc(planes_in[slot], 16)
                sp.dma_start(mixin[slot][3 * G:3 * G + NP, 0, :], scr_k[par, :, px])\
                  .then_inc(planes_in[slot], 16)

            def load_residual(n, s, slot):
                sp.dma_start(xres[slot][0:C], x_rows[n, :, bass.ds(s * PX, 2 * PX)])\
                  .then_inc(res_in[slot], 16)

            def store_channel(par, f, c, slot):
                sp.wait_ge(y_sb, done(f))
                sp.wait_ge(h_sb, done(f))
                sp.sem_inc(turns, 1)
                sp.dma_start(scr_img[par, c], planes_sb[slot]).then_inc(ch_out[slot], 16)

            def store_constants(m):
                sp.wait_ge(pl_sb, done(m))
                sp.sem_inc(turns, 1)
                sp.dma_start(scr_k_img[m % 2, :, 0:4, :], pimg[:, :, :]).then_inc(pl_out, 16)

            def store_pixels(n, s, slot):
                sp.wait_ge(px_sb, done(n * S + s + 1))
                sp.sem_inc(turns, 1)
                sp.dma_start(out_rows[n, :, bass.ds(s * PX, 2 * PX)], ost[slot][0:C])\
                  .then_inc(px_out[slot], 16)

            def sample(n, front, back, follows=False, ahead=True):
                m = n + 1 if back else n
                q = m + 1
                if front and ahead:
                    sp.wait_ge(piece_sb, q * PIECES)
                    sp.sem_inc(turns, 1)
                    load_stats(q, 0, 0)
                if back:
                    for k in range(2):
                        sp.wait_ge(ch_out[k], done(channel_use(n, S // GROUP - 1, GROUP - 2), 16))
                    sp.wait_ge(pl_out, done(n, 16))
                    load_planes(n % 2, 0, 0)

                def step(s, g, k):
                    slot = k // 2
                    b = n * S + s
                    if k % 2 == 0:
                        if not is_strip(s, S - 2):
                            if back:
                                load_pixels(n, s + 2, 1 - slot, last=is_strip(s, S - 4), now=b)
                                load_planes(n % 2, s + 2, 1 - slot)
                            if front:
                                load_raw(m, s + 2, 1 - slot)
                        elif front:
                            if ahead:
                                load_raw(m + 1, 0, 0)
                            load_pixels(m, 0, 0, first=True, now=b if back else None)
                        if back:
                            if follows or not (is_strip(s, 0) or is_strip(s, 2)):
                                sp.wait_ge(px_sb, done(b - 3))
                                sp.sem_inc(turns, 1)
                            load_residual(n, s, slot)
                    if front and ahead and k % 2 == 0 and not (isinstance(s, int) and s + 2 >= PIECES):
                        sp.wait_ge(piece_sb, q * PIECES + s)
                        sp.sem_inc(turns, 1)
                        load_stats(q, s_half(g, k) + 1, 1 - slot)
                    if front:
                        store_channel(m % 2, m * S + s, s, k % 2)
                        if is_strip(s, 0):
                            store_constants(m)
                    if back and is_strip(s, 1):
                        if follows:
                            store_pixels(n - 1, S - 2, 1)
                    elif back and k % 2 == 1:
                        store_pixels(n, s - 3, 1 - slot)
                strips(sp, step)

            load_raw(0, 0, 0, first=True)
            sample(0, True, False)
            sample(0, True, True)
            with sp.Fori(1, NS - 2) as n:
                sample(n, True, True, follows=True)
            sample(NS - 2, True, True, follows=True, ahead=False)
            sample(NS - 1, False, True, follows=True)
            store_pixels(NS - 1, S - 2, 1)
            for k in range(2):
                sp.wait_ge(ch_out[k], done(channel_use(NS - 1, S // GROUP - 1, GROUP - 2), 16))
                sp.wait_ge(px_out[k], done(pixel_use(NS - 1, S // GROUP - 1), 16))
            sp.wait_ge(pl_out, done(NS - 1, 16))

        @block.tensor
        def _(pe):
            mm = pe.matmul
            def group_means(q):
                ps = free_bank(MEANS)
                pe.wait_ge(mv_sb, q + 1)
                mm(ps[:, col["gm"]], means[:, 0:N], mean3[:, :], start=True, stop=True)
                for j in range(THIRDS):
                    mm(ps[0:C, col["chm"]], means[:, N + (j + 1) * C:N + (j + 2) * C], mv[:, j, 0:1],
                       start=(j == 0), stop=(j == THIRDS - 1))
                last = mm(ps[0:C, col["gmc"]], means[:, N:N + C], mean3[:, :], start=True, stop=True)
                last.then_inc(mean_ps, 1)

            def group_variances(q):
                ps = free_bank(VARIANCES)
                pe.wait_ge(dev_sb, q + 1)
                for j in range(THIRDS):
                    last = mm(ps[0:C, col["var"]], means[:, N:N + C], ssq[:, j:j + 1],
                              start=(j == 0), stop=(j == THIRDS - 1))
                last.then_inc(var_ps, 1)

            def first_layers(q):
                ps = free_bank(LAYERS)
                pe.wait_ge(gap_sb, q + 1)
                at0 = col["cst"].start
                for k in range(3):
                    mm(ps[:, at0 + 2 * k:at0 + 2 * k + 2], sel[:, k, :], t96[:, :], start=True, stop=True)
                mm(ps[0:NH, col["l1"]], mlp1[:, :], gap[:, :], start=True, stop=True)\
                    .then_inc(l1_ps, 1)

            def second_layers(q):
                ps = free_bank(SIGMOIDS)
                pe.wait_ge(hidw_sb, q + 1)
                mm(ps[:, col["l2"]], mlp2[:, :], hidb[:, :], start=True, stop=True)
                mm(ps[:, col["go"]], ones[0:NH, :], hidw[:, :], start=True, stop=True).then_inc(go_ps, 1)

            def constant_sums(q):
                ps = free_bank(SUMS)
                pe.wait_ge(mixw_sb, q + 1)
                mm(ps[C:C + NP, col["sums"]], bsel[0:C, :], new_freq[0:C, :], start=True, stop=True)
                mm(ps[2 * G:3 * G, col["bias"]], new_fft[0:C, :], bmir[0:C, :],
                   start=True, stop=True).then_inc(sums_ps, 1)

            pe.wait_ge(setup_in, 16 * len(set_loads))
            pe.wait_ge(consts_in, 16 * len(loads))
            pe.wait_ge(ones_sb, 1)
            for stage in (group_means, group_variances, first_layers, second_layers, constant_sums):
                stage(0)
            pe.wait_ge(credited, 1)

            def transforms_in(m, s, g, k):
                f, first, image = m * S + s, is_strip(s, 0), raw[slot_of(k)][:, 1, k % 2, :]
                if first:
                    pe.wait_ge(gl_sb, done(m))
                pe.wait_ge(xs_sb, done(f))
                pe.wait_ge(tl_sb, before(f))
                mm(ps_t[:, 0:2 * N], xhi[:, :], ghi[:, 1:3, :], start=True, stop=False)
                mm(ps_t[:, 0:2 * N], xhi[:, :], glo[:, 1:3, :], start=False, stop=False)
                mm(ps_t[:, 0:2 * N], xlo[:, :], ghi[:, 1:3, :], start=False, stop=True)\
                    .then_inc(t_ps, 1)
                pe.wait_ge(raw_in[slot_of(k)], uses(m, g) * 32)
                pe.wait_ge(ht_sb, before(f))
                if is_strip(s, 1):
                    pe.wait_ge(pl_sb, done(m))
                pe.transpose(ps_ht[:, 0:N], image, EYE)
                pe.transpose(ps_ht[:, N:2 * N], image, FLIP).then_inc(ht_ps, 1)

            def transforms_out(m, s):
                f = m * S + s
                if is_strip(s, 0):
                    pe.wait_ge(row_sb, done(m))
                pe.wait_ge(ht_sb, done(f))
                pe.wait_ge(h_sb, before(f))
                mm(ps_h[:, 0:N], htsb[:, 0, :], HT, start=True, stop=True)
                mm(ps_h[:, 2 * N:3 * N], htsb[:, 1, :], mats[:, 4, :], start=True, stop=True)
                pe.transpose(ps_h[:, N:2 * N], htsb[:, 1, :], FLIP).then_inc(h_ps, 1)
                pe.wait_ge(tl_sb, done(f))
                pe.wait_ge(y_sb, before(f))
                for part in range(2):
                    cut = slice(1 - part, 3 - part)
                    mm(ps_y[:, 0:2 * N], thi[:, part, :], ghi[:, cut, :],
                       start=(part == 0), stop=False)
                    mm(ps_y[:, 0:2 * N], thi[:, part, :], glo[:, cut, :], start=False, stop=False)
                    last = mm(ps_y[:, 0:2 * N], tlo[:, part, :], ghi[:, cut, :],
                              start=False, stop=(part == 1))
                last.then_inc(y_ps, 1)

            def first_conv(n, s):
                b = n * S + s
                if is_strip(s, 0):
                    pe.wait_ge(back_sb, done(n))
                pe.wait_ge(x0_sb, done(b))
                pe.wait_ge(c0_sb, before(b))
                for dw in range(3):
                    for p in range(2):
                        last = mm(ps_c0[p * 2 * G:(p + 1) * 2 * G, 0:N],
                                  cur_w0[:, dw].rearrange("p a b -> p (a b)"),
                                  x0[:, p, dw:dw + N], start=(dw == 0), stop=(dw == 2))
                last.then_inc(c0_ps, 1)

            def mixes(n, s, g, k):
                b, first, slot = n * S + s, is_strip(s, 0), slot_of(k)
                px = slice(k % 2 * PX, (k % 2 + 1) * PX)
                pe.wait_ge(mix_in[slot], uses(n, g) * 16)
                pe.wait_ge(planes_in[slot], uses(n, g) * 48)
                pe.wait_ge(sq_sb, before(b))
                pe.wait_ge(fft_sb, before(b))
                mm(ps_mix[2 * G:3 * G, :], cur_fft[:, :], mixin[slot][:, 1, px],
                   start=True, stop=not first)
                last = mm(ps_mix[0:2 * G, :], cur_freq[0:C + NP, :], mixin[slot][0:C + NP, 0, px],
                          start=True, stop=True)
                if first:
                    last = mm(ps_mix[2 * G:3 * G, 0:N], b1rows[:, :], row0[:, :],
                              start=False, stop=True)
                last.then_inc(mix_ps, 1)

            def window(k, which, row, col):
                return ring[:, which, k * ROWS + row:k * ROWS + row + ROWS, col:col + N]

            def acc(k):
                return strip(ps_c2[k % 2][0:C, :])

            def last_conv_begin(n, s, g, k, tail=False):
                b = n * S + s
                last_strip = is_strip(s, S - 1)
                pe.wait_ge(shift_sb, done(b if last_strip else b + 1))
                pe.wait_ge(lo_sb, done(b if last_strip else b + 1))
                if last_strip:
                    pe.wait_ge(border_sb, done(n))
                elif k == GROUP - 1:
                    pe.wait_ge(twin_sb, done(n * (S // GROUP) + g + 1))
                pe.wait_ge(px_sb, b if tail else before(b))
                for tap in range(9):
                    mm(acc(k), w2a[:, tap, :], window(k, 0, tap // 3, tap % 3),
                       start=(tap == 0), stop=False)

            def last_conv_end(n, s, g, k):
                for tap in range(9):
                    mm(acc(k), w2b[:, tap, :], window(k, 1, tap // 3, tap % 3), start=False, stop=False)
                for j, (corner, _) in enumerate(CORNERS):
                    last = mm(acc(k), w2c[:, j, :], window(k, 2, *corner),
                              start=False, stop=(j == len(CORNERS) - 1))
                last.then_inc(c2_ps, 1)

            def make_g(m):
                pe.wait_ge(tl_sb, done(m * S - 1))
                pe.wait_ge(el_sb, done(m))
                mm(ps_t[:, 0:2 * N], ET, el[:, :, :], start=True, stop=True).then_inc(g_ps, 1)

            def make_rows(m):
                pe.wait_ge(tab_sb, done(m))
                pe.wait_ge(y_sb, done(m * S - 1))
                pe.wait_ge(h_sb, done(m * S - 1))
                for k, bank in enumerate((ps_y, ps_h)):
                    for j, a in enumerate((0, 2, 1)):
                        last = mm(bank[0:2, j * N:(j + 1) * N], cur_tab[:, 4 * k + a:4 * k + a + 2],
                                  ET, start=True, stop=True)
                last.then_inc(row_ps, 1)

            def make_planes(m):
                pe.wait_ge(row_sb, done(m))
                pe.wait_ge(ht_sb, done(m * S))
                for k in range(2):
                    last = mm(ps_ht[:, k * 2 * N:(k + 1) * 2 * N], prow[:, k, 0, :],
                              prow[:, k, 1:3, :], start=True, stop=True)
                last.then_inc(pl_ps, 1)

            def sample(n, front, back, follows=False, ahead=True):
                m = n + 1 if back else n
                q, ahead = m + 1, ahead and front

                def conv_two_before(part, s, g, k):
                    j = (k - LAG) % GROUP
                    if is_strip(s, 0) or is_strip(s, 1):
                        if follows:
                            part(n - 1, S - LAG + s, S // GROUP - 1, j)
                    else:
                        part(n, s - LAG, g if k >= LAG else g - 1, j)

                def step(s, g, k):
                    late = is_strip(s, 0)
                    if back:
                        first_conv(n, s)
                        if not late and not is_strip(s, 1):
                            mixes(n, s, g, k)
                    if front and not late:
                        transforms_in(m, s, g, k)
                    if back and is_strip(s, 1):
                        mixes(n, s, g, k)
                    if ahead and is_strip(s, VARIANCES):
                        group_variances(q)
                    if ahead and is_strip(s, LAYERS):
                        first_layers(q)
                    if ahead and is_strip(s, SIGMOIDS):
                        if back:
                            pe.wait_ge(px_sb, done(n * S + s - 3))
                        second_layers(q)
                    if ahead and is_strip(s, MEANS + 1):
                        pe.wait_ge(dev_sb, q + 1)
                    if ahead and is_strip(s, VARIANCES + 1):
                        pe.wait_ge(veps_sb, q + 1)
                    if ahead and is_strip(s, SIGMOIDS + 1):
                        pe.wait_ge(logit_sb, q + 1)
                    if ahead and is_strip(s, SUMS + 1):
                        pe.wait_ge(new_sb, q + 1)
                    if back:
                        conv_two_before(last_conv_begin, s, g, k)
                    if front and late:
                        make_rows(m)
                        transforms_in(m, s, g, k)
                    if back and late:
                        conv_two_before(last_conv_end, s, g, k)
                        mixes(n, s, g, k)
                    if front:
                        transforms_out(m, s)
                        if late:
                            make_planes(m)
                    if back and not late:
                        conv_two_before(last_conv_end, s, g, k)
                    if ahead and is_strip(s, MEANS):
                        group_means(q)
                    if ahead and is_strip(s, SUMS):
                        constant_sums(q)
                strips(pe, step)
                if ahead:
                    make_g(q)

            make_g(0)
            sample(0, True, False)
            sample(0, True, True)
            with pe.Fori(1, NS - 2) as n:
                sample(n, True, True, follows=True)
            sample(NS - 2, True, True, follows=True, ahead=False)
            sample(NS - 1, False, True, follows=True)
            for k in range(LAG, GROUP):
                last_conv_begin(NS - 1, S - GROUP + k, S // GROUP - 1, k, tail=True)
                last_conv_end(NS - 1, S - GROUP + k, S // GROUP - 1, k)

        @block.scalar
        def _(act):
            act.wait_ge(setup_in, 16 * len(set_loads))
            act.activation(w2a[:, :, :], w2raw, ACT.Copy)
            act.activation(w2b[C:N, :, :], w2braw[C:N], ACT.Copy)
            act.activation(table_load[:, :], mlp1b[0:1, 0:1], ACT.Square)
            act.activation(w2c[:, :, :], w2craw, ACT.Copy).then_inc(w2hi_sb, 1)

            def deviations(q):
                act.wait_ge(veps_sb, q + 1)
                act.activation(sd[:, :], sd[:, :], ACT.Sqrt).then_inc(sd_sb, 1)

            def sigmoids(q):
                act.wait_ge(logit_sb, q + 1)
                act.activation(gates[:, :], gates[:, :], ACT.Sigmoid).then_inc(gate_sb, 1)

            def sines(q):
                act.wait_ge(turn_sb, q + 1)
                act.activation(trig[:, :], turn[:, :], ACT.Sin, scale=TWO_PI).then_inc(trig_sb, 1)

            for stage in (deviations, sigmoids, sines):
                stage(0)
            act.wait_ge(credited, 1)

            def copy_g(m):
                act.wait_ge(g_ps, done(m))
                act.activation(ghi[:, 1:3, :], ps_t[:, 0:2 * N], ACT.Copy)
                act.activation(ghi[:, 0, :], ps_t[:, N:2 * N], ACT.Copy, scale=-1.0)\
                   .then_inc(gh_sb, 1)

            def sample(n, front, back, ahead=True):
                m = n + 1 if back else n
                q, ahead = m + 1, ahead and front

                def normalise(n, s, g, k):
                    b, src = n * S + s, x0raw[slot_of(k)][:, k % 2 * 2:k % 2 * 2 + 2, :]
                    first, last = is_strip(s, 0), is_strip(s, S - 1)
                    if first:
                        act.wait_ge(back_sb, done(n))
                    act.wait_ge(x0_in[slot_of(k)], uses(n, g) * 64)
                    act.wait_ge(c0_ps, before(b))
                    if first or last:
                        for p in range(2):
                            v = 1 if first and p == 0 else 2 if last and p == 1 else 0
                            op = act.activation(x0[:, p, 1:N + 1], src[:, p, :],
                                                ACT.Identity, bias=cur_rb[:, v, 1:2],
                                                scale=cur_rb[:, v, 0:1])
                    else:
                        op = act.activation(x0[:, :, 1:N + 1], src, ACT.Identity,
                                            bias=cur_rb[:, 0, 1:2], scale=cur_rb[:, 0, 0:1])
                    op.then_inc(x0_sb, 1)

                def squares(b):
                    act.wait_ge(mix_ps, done(b))
                    act.wait_ge(sum_sb, before(b))
                    act.activation(sq[G:2 * G, 0, :], ps_mix[0:G, :], ACT.Square)
                    act.activation(sq[G:2 * G, 1, :], ps_mix[G:2 * G, :], ACT.Square)\
                       .then_inc(sq_sb, 1)

                def high_t(f):
                    act.wait_ge(t_ps, done(f))
                    act.wait_ge(y_ps, before(f))
                    act.activation(thi[:, :, :], ps_t[:, 0:2 * N], ACT.Copy).then_inc(th_sb, 1)

                def high_parts(b, k):
                    act.wait_ge(sum_sb, done(b))
                    act.wait_ge(lo_sb, before(b))
                    act.activation(mixed[G:2 * G], sq[G:2 * G, 0, :], ACT.Sqrt)\
                       .then_inc(abs_sb, 1)
                    act.wait_ge(c0_sb, done(b))
                    act.wait_ge(fft_sb, done(b))
                    act.wait_ge(abs_sb, done(b))
                    both = ring[0:C, 0:2, k * ROWS + 1:k * ROWS + 1 + ROWS, 1:N + 1]
                    act.activation(both, strip(mixed[0:C])[:, None].to_broadcast([C, 2, ROWS, N]),
                                   ACT.Copy)\
                       .then_inc(hi_sb, 1)

                def step(s, g, k):
                    b, f = n * S + s, m * S + s
                    late = is_strip(s, 0)
                    if back and late:
                        act.activation(table_load[0:1, :], table_load[0:1, :], ACT.Sqrt)
                    if back and is_strip(s, 1):
                        normalise(n, 2, 0, 2)
                    if back and not (late or is_strip(s, 1) and front):
                        squares(b)
                    if front and not (back and is_strip(s, 1)):
                        high_t(f)
                    if back and not late:
                        high_parts(b, k)
                    if back and late:
                        normalise(n, 1, 0, 1)
                        squares(b)
                    if front:
                        act.wait_ge(ch_out[k % 2], before(channel_use(m, g, k), 16))
                        act.wait_ge(h_ps, done(f))
                        act.activation(planes_sb[k % 2][:, 2:5, :], ps_h[:, 0:3 * N], ACT.Copy)\
                           .then_inc(h_sb, 1)
                        act.wait_ge(y_ps, done(f))
                        act.activation(planes_sb[k % 2][:, 0:2, :], ps_y[:, 0:2 * N], ACT.Copy)\
                           .then_inc(y_sb, 1)
                    if back and late:
                        if front:
                            high_t(f + 1)
                        high_parts(b, k)
                        if front:
                            squares(b + 1)
                    elif back and not (is_strip(s, 1) or is_strip(s, S - 1)):
                        normalise(n, s + 1, g if k < GROUP - 1 else g + 1, (k + 1) % GROUP)
                    elif back and front and is_strip(s, S - 1):
                        normalise(n + 1, 0, 0, 0)
                    if back:
                        act.wait_ge(lo2_sb, done(b))
                        src = ring32[0:G, 2, k * ROWS + 1:k * ROWS + 1 + ROWS, :]
                        act.activation(ring[2 * G:3 * G, 2, k * ROWS + 1:k * ROWS + 1 + ROWS, 0:N - 1],
                                       src[:, :, 2:N + 1], ACT.Copy)
                        act.activation(ring[3 * G:4 * G, 2, k * ROWS:k * ROWS + ROWS, 1:N + 1],
                                       src[:, :, 1:N + 1], ACT.Copy).then_inc(shift_sb, 1)
                    if ahead and is_strip(s, VARIANCES):
                        deviations(q)
                    if ahead and is_strip(s, SIGMOIDS):
                        sigmoids(q)
                    if ahead and is_strip(s, SINES):
                        sines(q)
                strips(act, step)
                if front and not back:
                    normalise(0, 0, 0, 0)
                if ahead:
                    copy_g(q)

            copy_g(0)
            sample(0, True, False)
            with act.Fori(0, NS - 2) as n:
                sample(n, True, True)
            sample(NS - 2, True, True, ahead=False)
            sample(NS - 1, False, True)

        @block.gpsimd
        def _(pool):
            pool.memset(ring32, 0.0).then_inc(border, 1)
            pool.wait_ge(credited, 1)

            def sample(n, front, back):
                m = n + 1 if back else n

                def split(s, g, k, pixels):
                    f, image = m * S + s, raw[slot_of(k)][:, 0, k % 2, :]
                    pool.wait_ge(raw_in[slot_of(k)], uses(m, g) * 32)
                    pool.wait_ge(t_ps, before(f))
                    pool.wait_ge(xs_sb, before(f))
                    if pixels is not None:
                        pool.wait_ge(sum_sb, done(pixels))
                    pool.sem_inc(turns, 1)
                    pool.tensor_copy(xhi[:, :], image).then_inc(xh_sb, 1)
                    pool.wait_ge(xh_sb, done(f))
                    pool.tensor_tensor(xlo[:, :], image, xhi[:, :].bitcast(F32),
                                       ALU.subtract).then_inc(xs_sb, 1)

                def step(s, g, k):
                    b = n * S + s
                    if front and not (back and is_strip(s, 1)):
                        split(s, g, k, b - 1 if back else None)
                    if front and back and is_strip(s, 0):
                        split(s + 1, g, k + 1, b - 1)
                    if back:
                        pool.wait_ge(sq_sb, done(b))
                        pool.wait_ge(abs_sb, before(b))
                        if front:
                            pool.wait_ge(xs_sb, done(m * S + s + (1 if is_strip(s, 0) else 0)))
                        pool.wait_ge(sum_sb, before(b))
                        pool.tensor_tensor(sq[G:2 * G, 0, :], sq[G:2 * G, 0, :], sq[G:2 * G, 1, :],
                                           ALU.add).then_inc(sum_sb, 1)
                strips(pool, step)

            sample(0, True, False)
            with pool.Fori(0, NS - 1) as n:
                sample(n, True, True)

        @block.vector
        def _(dve):
            tt, ts, stt, cp = dve.tensor_tensor, dve.tensor_scalar, dve.scalar_tensor_tensor, dve.tensor_copy
            links, linked = 16, [0]

            def link(q, op):
                linked[0] += 1
                assert linked[0] <= links
                op.then_inc(link_sb, 1)
                dve.wait_ge(link_sb, q * links + linked[0])

            def piece(q, s, g, k):
                dve.wait_ge(stat_in[k // 2], (q * STATS_GROUPS + (g + 1)) * 16)
                dve.bn_stats(stats[:, bass.ds(s, 1), :].rearrange("p a b -> p (a b)"),
                             stat_raw[k // 2][:, k % 2 * PIECE:(k % 2 + 1) * PIECE])\
                   .then_inc(piece_sb, 1)

            def thirds(q):
                dve.wait_ge(piece_sb, (q + 1) * PIECES)
                dve.sem_inc(turns, 1)
                for j in range(THIRDS):
                    op = dve.bn_aggr(mv[:, j, :], stats[:, 8 * j:8 * j + 8, :])
                linked[0] = 0
                link(q, op)
                link(q, tt(mean3[:, :], mv[:, 0, 0:1], mv[:, 1, 0:1], ALU.add))
                tt(mean3[:, :], mean3[:, :], mv[:, 2, 0:1], ALU.add).then_inc(mv_sb, 1)

            def deviations(q):
                ps = free_bank(MEANS)
                dve.wait_ge(mean_ps, q + 1)
                cp(gm[:, :], ps[:, col["gm"]])
                link(q, cp(chm[:, :], ps[0:C, col["chm"].start:col["gmc"].stop]))
                link(q, ts(dev[:, :], mv[:, :, 0], gm[:, 0:1], None, ALU.subtract))
                link(q, tt(ssq[:, :], dev[:, :], dev[:, :], ALU.mult))
                tt(ssq[:, :], ssq[:, :], mv[:, :, 1], ALU.add).then_inc(dev_sb, 1)

            def plus_epsilon(q):
                ps = free_bank(VARIANCES)
                dve.wait_ge(var_ps, q + 1)
                ts(sd[:, :], ps[0:C, col["var"]], EPS, None, ALU.add).then_inc(veps_sb, 1)

            def scales(q):
                dve.wait_ge(sd_sb, q + 1)
                link(q, dve.reciprocal(t96[:, 0:1], sd[:, :]))
                link(q, tt(gap[:, :], chm[:, 0:1], chm[:, 1:2], ALU.subtract))
                stt(t96[:, 1:2], chm[:, 1:2], -1.0, t96[:, 0:1], ALU.mult, ALU.mult)
                tt(gap[:, :], gap[:, :], t96[:, 0:1], ALU.mult).then_inc(gap_sb, 1)

            def hidden_weighted(q):
                ps = free_bank(LAYERS)
                dve.wait_ge(l1_ps, q + 1)
                cp(cst[:, :, :].rearrange("p a b -> p (a b)"), ps[:, col["cst"]])
                link(q, tt(hid[:, :], ps[0:NH, col["l1"]], mlp1b[:, :], ALU.add))
                link(q, ts(hid[:, :], hid[:, :], 0.0, None, ALU.max))
                ts(hidb[:, :], own[:, :], hid[:, 0:1], None, ALU.mult)
                ts(hidw[:, :], mlpgo[:, :], hid[:, 0:1], None, ALU.mult).then_inc(hidw_sb, 1)

            def logits(q):
                ps = free_bank(SIGMOIDS)
                dve.wait_ge(go_ps, q + 1)
                link(q, cp(gi[:, :], ps[:, col["l2"]]))
                cp(gates[:, 9 * G:9 * G + 1], gi[:, 0:1])
                go = col["go"].start
                for j, k in enumerate((0, 0, 1, 1, 2)):
                    a, z = GATE_COLS[k]
                    op = ts(gates[:, 2 * G * j:2 * G * j + z - a], ps[:, go + a:go + z],
                            gi[:, j + 1:j + 2], None, ALU.mult)
                op.then_inc(logit_sb, 1)

            def turns_of(q):
                dve.wait_ge(gate_sb, q + 1)
                link(q, ts(angle[:, :], gates[:, 9 * G:9 * G + 1], 0.8, 0.1, ALU.mult, ALU.add))
                link(q, stt(turn[:, :], cols[:, 0:4], angle[:, 0:1], cols[:, 8:12], ALU.mult, ALU.add))
                link(q, ts(whole[:, :], turn[:, :], ROUND, None, ALU.add))
                link(q, ts(whole[:, :], whole[:, :], ROUND, None, ALU.subtract))
                tt(turn[:, :], turn[:, :], whole[:, :], ALU.subtract).then_inc(turn_sb, 1)

            def mixing_weights(q):
                link(q, stt(gates[:, 0:8 * G], gates[:, 0:8 * G], 0.5,
                            w_mix[:, :, :].rearrange("p a b -> p (a b)"), ALU.mult, ALU.mult))
                p = [slice(a * G, (a + 1) * G) for a in range(4)]
                A, Cw, B, D = (gates[:, a * G:(a + 1) * G] for a in range(4))
                lo, hi = slice(0, G), slice(G, 2 * G)
                tt(new_freq[p[0], lo], A[p[0]], D[p[0]], ALU.add)
                tt(new_freq[p[0], hi], Cw[p[0]], B[p[0]], ALU.subtract)
                tt(new_freq[p[1], lo], A[p[1]], D[p[1]], ALU.subtract)
                tt(new_freq[p[1], hi], B[p[1]], Cw[p[1]], ALU.add)
                stt(new_freq[p[2], lo], B[p[2]], -1.0, Cw[p[2]], ALU.mult, ALU.subtract)
                op = tt(new_freq[p[2], hi], A[p[2]], D[p[2]], ALU.subtract)
                op.then_inc(link_sb, 1)

            def fft_weights(q):
                dve.wait_ge(link_sb, (q + 1) * links)
                p = [slice(a * G, (a + 1) * G) for a in range(4)]
                A, Cw, B, D = (gates[:, a * G:(a + 1) * G] for a in range(4, 8))
                tt(new_fft[p[0], :], A[p[0]], D[p[0]], ALU.add)
                tt(new_fft[p[1], :], B[p[1]], Cw[p[1]], ALU.subtract)
                tt(new_fft[p[2], :], A[p[2]], D[p[2]], ALU.subtract)
                tt(new_fft[p[3], :], B[p[3]], Cw[p[3]], ALU.add)
                ts(bsel[:, :], cols[:, 20:20 + NP], cst[:, 1, 1:2], None, ALU.mult)
                ts(bmir[:, :], cols[:, 25:26], cst[:, 2, 1:2], None, ALU.mult).then_inc(mixw_sb, 1)

            def scaled_weights(q):
                ps = free_bank(SUMS)
                dve.wait_ge(sums_ps, q + 1)
                tt(new_freq[C:C + NP, :], ps[C:C + NP, col["sums"]], brow[C:C + NP, :], ALU.add)
                cp(new_bias[2 * G:3 * G, :], ps[2 * G:3 * G, col["bias"]])
                ts(new_freq[0:C, :], new_freq[0:C, :], cst[0:C, 1, 0:1], None, ALU.mult)
                ts(new_fft[:, :], new_fft[:, :], cst[:, 2, 0:1], None, ALU.mult).then_inc(new_sb, 1)

            def keep_weights(m):
                dve.wait_ge(new_sb, m + 1)
                cp(next_freq[0:C + NP, :], new_freq[0:C + NP, :])
                cp(next_fft[:, :], new_fft[:, :])
                cp(next_bias[2 * G:3 * G, :], new_bias[2 * G:3 * G, :])
                cp(next_rb[:, :], cst[:, 0, :])
                cp(next_w0[:, :], gates[:, 8 * G:9 * G]).then_inc(next_sb, 1)

            def start_linked(op, count):
                op.then_inc(start_link, 1)
                dve.wait_ge(start_link, count)

            start_linked(dve.memset(ones[:, :], 1.0), 1)
            dve.sem_inc(ones_sb, 1)
            for j in range(PIECES):
                piece(0, j, j // GROUP, j % GROUP)
            dve.wait_ge(setup_in, 16 * len(set_loads))
            dve.wait_ge(consts_in, 16 * len(loads))
            tt(brow[C:N, :], b05rows[C:N, :], sgn[C:N, :], ALU.mult).then_inc(brow_sb, 1)
            dve.wait_ge(brow_sb, 1)
            for stage in (thirds, deviations, plus_epsilon, scales, hidden_weighted, logits, turns_of,
                          mixing_weights, fft_weights):
                stage(0)
            dve.wait_ge(w2hi_sb, 1)
            start_linked(tt(w2b[0:C, :, :], w2raw[0:C], w2a[0:C, :, :].bitcast(F32), ALU.subtract), 2)
            dve.wait_ge(ones_out, 32)
            start_linked(dve.memset(x0, 0.0), 3)
            start_linked(dve.memset(x0raw[0], 0.0), 4)
            scaled_weights(0)
            dve.wait_ge(border, 1)
            for s_, v in credits:
                dve.sem_inc(s_, v)
            dve.sem_inc(credited, 1)

            def table(m):
                dve.wait_ge(trig_sb, m + 1)
                dve.wait_ge(row_ps, before(m))
                tt(cur_tab[:, 0:8].rearrange("p (a b c) -> p a b c", a=2, b=2),
                   cols[:, 12:20].rearrange("p (a b c) -> p a b c", a=2, b=2),
                   trig[:, :].rearrange("p (a c) -> p a c", a=2)[:, :, None, :].to_broadcast([N, 2, 2, 2]),
                   ALU.mult)
                cp(cur_tab[:, 8:10], trig[:, 0:2]).then_inc(tab_sb, 1)

            def scaled_vectors(m):
                dve.wait_ge(tab_sb, done(m))
                dve.wait_ge(g_ps, before(m))
                for j in range(2):
                    op = ts(el[:, j, :], ET, cur_tab[:, 8 + j:9 + j], None, ALU.mult)
                op.then_inc(el_sb, 1)

            def plane_rows(m):
                dve.wait_ge(row_ps, done(m))
                dve.wait_ge(pl_ps, before(m))
                for k, bank in enumerate((ps_y, ps_h)):
                    op = cp(prow[:, k].rearrange("p a b -> p (a b)"), bank[0:2, 0:3 * N])
                op.then_inc(row_sb, 1)

            def planes(m):
                dve.wait_ge(pl_ps, done(m))
                dve.wait_ge(pl_out, before(m, 16))
                cp(pimg[:, :, :].rearrange("p a b -> p (a b)"), ps_ht[:, :]).then_inc(pl_sb, 1)

            def weights(n):
                dve.wait_ge(c0_ps, before(n * S))
                dve.wait_ge(mix_ps, before(n * S))
                dve.wait_ge(x0_sb, before(n * S))
                dve.wait_ge(fft_sb, before(n * S))
                dve.wait_ge(next_sb, n + 1)
                cp(cur_freq[0:C + NP, :], next_freq[0:C + NP, :])
                cp(cur_fft[:, :], next_fft[:, :])
                cp(cur_bf[2 * G:3 * G, :], next_bias[2 * G:3 * G, :])
                cp(cur_rb[:, 0, :], next_rb[:, :])
                for k in range(2):
                    ts(cur_rb[:, 1 + k, :], next_rb[:, :], cols[:, 6 + k:7 + k], None, ALU.mult)
                for dw in range(3):
                    op = tt(cur_w0[:, dw], w0l[:, dw],
                            next_w0[:, None, :].to_broadcast([N, 2, G]), ALU.mult)
                op.then_inc(back_sb, 1)

            def low_g(m):
                dve.wait_ge(gh_sb, done(m))
                tt(glo[:, 1:3, :], ps_t[:, 0:2 * N].rearrange("p (a b) -> p a b", a=2),
                   ghi[:, 1:3, :].bitcast(F32), ALU.subtract)
                stt(glo[:, 0, :], ps_t[:, N:2 * N], -1.0, ghi[:, 0, :].bitcast(F32),
                    ALU.mult, ALU.subtract).then_inc(gl_sb, 1)

            def last_conv(n, s, g, k):
                b, slot, half = n * S + s, slot_of(k), slice(k % 2 * PX, (k % 2 + 1) * PX)
                dve.wait_ge(c2_ps, done(b))
                dve.wait_ge(res_in[slot], uses(n, g) * 16)
                if k % 2 == 0:
                    dve.wait_ge(px_out[slot], before(pixel_use(n, g), 16))
                stt(ost[slot][0:C, half], ps_c2[k % 2][0:C, :], b2c[:, 0:1], xres[slot][0:C, half],
                    ALU.add, ALU.add).then_inc(px_sb, 1)

            def sample(n, front, back, follows=False, ahead=True):
                m = n + 1 if back else n
                q, ahead = m + 1, ahead and front

                def fft_strip(b):
                    dve.wait_ge(mix_ps, done(b))
                    ts(mixed[2 * G:3 * G], ps_mix[2 * G:3 * G, :], cur_bf[2 * G:3 * G, 0:1], None,
                       ALU.add).then_inc(fft_sb, 1)

                def add_squares(b):
                    dve.wait_ge(sq_sb, done(b))
                    dve.wait_ge(abs_sb, before(b))
                    tt(sq[G:2 * G, 0, :], sq[G:2 * G, 0, :], sq[G:2 * G, 1, :], ALU.add)\
                      .then_inc(sum_sb, 1)

                def low_parts(b, k):
                    dve.wait_ge(hi_sb, done(b))
                    p = slice(2 * G, 3 * G)
                    hi = rows(2 * G, 3 * G, 0, k).bitcast(F32)
                    tt(rows(0, G, 2, k), strip(mixed[p]), hi, ALU.subtract).then_inc(lo2_sb, 1)
                    tt(ring[G:2 * G, 2, k * ROWS + 1:k * ROWS + 1 + ROWS, 0:N], strip(mixed[p]),
                       hi, ALU.subtract)
                    for q in range(2):
                        op = tt(rows(3 * G, 4 * G, q, k), strip(mixed[q * G:(q + 1) * G]),
                                rows(q * G, (q + 1) * G, 0, k).bitcast(F32), ALU.subtract)
                    op.then_inc(lo_sb, 1)

                def transposed(f):
                    dve.wait_ge(ht_ps, done(f))
                    dve.wait_ge(h_ps, before(f))
                    cp(htsb.rearrange("p a b -> p (a b)"), ps_ht[:, 0:2 * N]).then_inc(ht_sb, 1)
                    dve.wait_ge(th_sb, done(f))
                    tt(tlo[:, :, :], ps_t[:, 0:2 * N].rearrange("p (a b) -> p a b", a=2),
                       thi[:, :, :].bitcast(F32), ALU.subtract).then_inc(tl_sb, 1)

                def step(s, g, k):
                    b, f = n * S + s, m * S + s
                    late = is_strip(s, 0)
                    if back:
                        dve.wait_ge(c0_ps, done(b))
                        dve.wait_ge(hi_sb, before(b))
                        dve.wait_ge(lo_sb, before(b))
                        for r in range(ROWS):
                            p = slice(r * G, (r + 1) * G)
                            op = ts(mixed[0:G, r * N:(r + 1) * N], ps_c0[p, 0:N], b0c[p, 0:1], None,
                                    ALU.add)
                        op.then_inc(c0_sb, 1)
                        if not front:
                            add_squares(b)
                        if not late or not front:
                            fft_strip(b)
                    if front and late:
                        plane_rows(m)
                    if front and not (back and is_strip(s, 1)):
                        transposed(f)
                    if ahead and not (isinstance(s, int) and s >= PIECES):
                        piece(q, s, g, k)
                    if ahead and is_strip(s, MEANS):
                        thirds(q)
                    if ahead and is_strip(s, VARIANCES):
                        plus_epsilon(q)
                    if ahead and is_strip(s, LAYERS):
                        hidden_weighted(q)
                    if ahead and is_strip(s, SIGMOIDS):
                        logits(q)
                    if ahead and is_strip(s, SINES):
                        mixing_weights(q)
                    if ahead and is_strip(s, SUMS):
                        fft_weights(q)
                    if front and is_strip(s, S - 1):
                        weights(m)
                    if back and not late:
                        low_parts(b, k)
                    j = (k - LAG) % GROUP
                    if is_strip(s, 0) or is_strip(s, 1):
                        if follows:
                            last_conv(n - 1, S - LAG + s, S // GROUP - 1, j)
                    elif back:
                        last_conv(n, s - LAG, g if k >= LAG else g - 1, j)
                    if back and front and late:
                        fft_strip(b)
                    if front and late:
                        planes(m)
                    if back and late:
                        if front:
                            transposed(f + 1)
                        low_parts(b, k)
                    if back:
                        if is_strip(s, 0):
                            dve.sem_inc(twin_sb, 1)
                        elif k == 0:
                            dve.wait_ge(shift_sb, done(b))
                            dve.wait_ge(lo_sb, done(b))
                            cp(ring[:, :, RING - 1, :], ring32[:, :, 1, :]).then_inc(twin_sb, 1)
                        elif is_strip(s, S - 1):
                            dve.wait_ge(shift_sb, done(b))
                            dve.wait_ge(lo_sb, done(b))
                            dve.memset(ring32[:, :, 0:RING:RING - 1, :], 0.0).then_inc(border_sb, 1)
                        elif k == GROUP - 1:
                            dve.wait_ge(shift_sb, done(b))
                            dve.wait_ge(lo_sb, done(b))
                            cp(ring[:, :, 0, :], ring32[:, :, RING - 2, :])
                    if front and is_strip(s, 3):
                        keep_weights(m)
                    if ahead and is_strip(s, MEANS):
                        deviations(q)
                    if ahead and is_strip(s, VARIANCES):
                        scales(q)
                    if ahead and is_strip(s, SIGMOIDS):
                        turns_of(q)
                    if ahead and is_strip(s, SINES):
                        table(q)
                        scaled_vectors(q)
                    if ahead and is_strip(s, SUMS):
                        scaled_weights(q)
                strips(dve, step)
                if ahead:
                    low_g(q)

            table(0)
            scaled_vectors(0)
            low_g(0)
            sample(0, True, False)
            sample(0, True, True)
            with dve.Fori(1, NS - 2) as n:
                sample(n, True, True, follows=True)
            sample(NS - 2, True, True, follows=True, ahead=False)
            sample(NS - 1, False, True, follows=True)
            for k in range(LAG, GROUP):
                last_conv(NS - 1, S - GROUP + k, S // GROUP - 1, k)


def lay_out(inputs):
    w = {k.replace("L0_conv_", ""): np.asarray(v) for k, v in inputs.items() if k != "x"}
    f32 = np.float32
    p = np.arange(N) % G

    def gated(conv):
        t = conv[:, :, 0, 0]
        return np.stack([t[:, v * G + p].T for v in range(2)], axis=1)

    w0l = np.zeros((4, G, 3, 2, G), f32)
    for r in range(4):
        for q in range(2):
            if 0 <= r - q <= 2:
                w0l[r, :, :, q, :] = w["conv0_w"][:, :, r - q, :].transpose(1, 2, 0)
    inputs_at = {"alpha": G, "gfreq": G, "gfft": 2 * G, "gsp": 0}
    outputs = (0 * p, 2 * G + p, 3 * G + p, 2 * G + p, 3 * G + p, G + p)
    mlp1, mlp1b = np.zeros((C, NH), f32), np.ones((NH, 1), f32)
    mlp2, mlpgo = np.zeros((NH, N), f32), np.zeros((NH, 5 * G), f32)

    def second(name, feature):
        return np.concatenate([w[name + "_w2"][feature].T, w[name + "_b2"][None, feature]])

    for j, (name, feature) in enumerate(zip(BLOCKS, outputs)):
        a, z = j * UNITS, (j + 1) * UNITS
        mlp1[inputs_at[name]:inputs_at[name] + G, a:z - 1] = w[name + "_w1"].T
        mlp1b[a:z - 1, 0] = w[name + "_b1"]
        mlp2[a:z] = second(name, feature)
    for j, at, width in ((1, 0, 2 * G), (3, 2 * G, 2 * G), (5, 4 * G, G)):
        mlpgo[j * UNITS:(j + 1) * UNITS, at:at + width] = second(BLOCKS[j], np.arange(width))
    w2l = w["conv2_w"].transpose(1, 2, 3, 0).reshape(C, 9, C)
    w2c = np.zeros((4, G, len(CORNERS), C), f32)
    for j, ((row, col), groups) in enumerate(CORNERS):
        for q in groups:
            w2c[q, :, j, :] = w2l[2 * G:, 3 * (row + SHIFTS[q][0]) + col + SHIFTS[q][1], :]
    b05rows = np.zeros((N, 2 * G), f32)
    b05rows[98] = w["conv05_b"]
    b05rows[99, 0:G] = w["conv05_b"][G:]
    b05rows[99, G:] = w["conv05_b"][:G]
    return {
        "w0l": w0l.reshape(N, 3, 2, G), "w2a": np.concatenate([w2l, w2l[0:G]]), "w2b": w2l[G:2 * G],
        "w2c": w2c.reshape(N, len(CORNERS), C),
        "b0c": w["conv0_b"][p][:, None], "b2c": w["conv2_b"][:, None],
        "b1rows": w["conv1_b"].reshape(2, G),
        "w_mix": np.concatenate([gated(w["conv05_w"]), gated(w["conv1_w"])], axis=1),
        "b05rows": b05rows, "mlp1": mlp1, "mlp1b": mlp1b,
        "mlp2": mlp2, "mlpgo": mlpgo,
    }


def kernel(**inputs):
    import concourse.bacc as bacc
    from concourse.bass_utils import run_bass_kernel_spmd

    nc = bacc.Bacc("TRN2", target_bir_lowering=False, num_devices=1)
    x = np.ascontiguousarray(inputs["x"])
    arrays = {"x": x}
    arrays.update(constants())
    arrays.update({k: np.ascontiguousarray(v) for k, v in lay_out(inputs).items()})
    aps = {k: nc.dram_tensor("in_" + k, a.shape, mybir.dt.from_np(a.dtype), kind="ExternalInput").ap()
           for k, a in arrays.items()}
    out = nc.dram_tensor("out", x.shape, mybir.dt.from_np(x.dtype), kind="ExternalOutput").ap()
    build(nc, aps.pop("x"), out, aps)
    arrays = {"in_" + k: a for k, a in arrays.items()}
    r = run_bass_kernel_spmd(nc, [arrays], core_ids=[0])
    return r.results[0]["out"]
```
